# Optimizing a Trainium2 kernel written in Bass

```python
import numpy as np
import jax
import jax.numpy as jnp

def _softmax(x, axis=-1):
    return jax.nn.softmax(x, axis=axis)

def _gelu(x):
    return jax.nn.gelu(x, approximate=True)

def _silu(x):
    return jax.nn.silu(x)

def _sigmoid(x):
    return jax.nn.sigmoid(x)

def _layernorm(x, axis=-1, eps=1e-05):
    m = jnp.mean(x, axis=axis, keepdims=True)
    v = jnp.var(x, axis=axis, keepdims=True)
    return (x - m) / jnp.sqrt(v + eps)

def _scatter_add(tgt, idx, src, axis=0):
    return tgt.at[idx].add(src)

def _segment_sum(src, seg, n):
    return jax.ops.segment_sum(src, seg, n)
kernel_name = 'mk_adaln_d2_jaxref_r8_daa2c0'

def setup_inputs(seed: int=0):
    np.random.seed(seed)
    _w = jnp.asarray

    def _L0_attn_setup():
        import jax, jax.numpy as jnp
        import numpy as np
        B, S, DIM = (1, 256, 256)
        HEADS, KV_HEADS = (32, 8)
        DH = DIM // HEADS
        G = HEADS // KV_HEADS
        CBLK = 16
        SBLK = 16
        NSEL = 8
        WIN = 64
        SCALE = DH ** (-0.5)
        NEG = -1e+30
        CDIM = CBLK * DH

        def _rope(x, pos):
            d = x.shape[-1]
            inv = 1.0 / 10000.0 ** (jnp.arange(0, d, 2, dtype=jnp.float32) / d)
            ang = pos[:, None] * inv[None, :]
            cos, sin = (jnp.cos(ang), jnp.sin(ang))
            x1, x2 = (x[..., 0::2], x[..., 1::2])
            return jnp.stack([x1 * cos - x2 * sin, x1 * sin + x2 * cos], axis=-1).reshape(x.shape)

        def _forward(x, w_qkv, k_pos, v_pos, k_cw1, k_cb1, k_cw2, k_cb2, v_cw1, v_cb1, v_cw2, v_cb2, mem_ck, mem_cv, w_gate, b_gate, w_out):
            b, n, _ = x.shape
            di, dkv = (HEADS * DH, KV_HEADS * DH)
            qkv = x @ w_qkv
            q = qkv[..., :di].reshape(b, n, KV_HEADS, G, DH).transpose(0, 2, 3, 1, 4)
            k = qkv[..., di:di + dkv].reshape(b, n, KV_HEADS, DH).transpose(0, 2, 1, 3)
            v = qkv[..., di + dkv:].reshape(b, n, KV_HEADS, DH).transpose(0, 2, 1, 3)
            nc = n // CBLK
            kb = k[:, :, :nc * CBLK].reshape(b, KV_HEADS, nc, CBLK, DH) + k_pos[None, :, None]
            vb = v[:, :, :nc * CBLK].reshape(b, KV_HEADS, nc, CBLK, DH) + v_pos[None, :, None]
            ck = jax.nn.relu(kb.reshape(b, KV_HEADS, nc, CDIM) @ k_cw1 + k_cb1) @ k_cw2 + k_cb2
            cv = jax.nn.relu(vb.reshape(b, KV_HEADS, nc, CDIM) @ v_cw1 + v_cb1) @ v_cw2 + v_cb2
            ck = jnp.concatenate([jnp.broadcast_to(mem_ck[None], (b, KV_HEADS, 1, DH)), ck], axis=2)
            cv = jnp.concatenate([jnp.broadcast_to(mem_cv[None], (b, KV_HEADS, 1, DH)), cv], axis=2)
            csim = jnp.einsum('bhgnd,bhjd->bhgnj', q, ck) * SCALE
            ck_last = jnp.concatenate([jnp.array([-1]), (jnp.arange(nc) + 1) * CBLK - 1])
            cmask = ck_last[None, :] < jnp.arange(n)[:, None]
            csim = jnp.where(cmask, csim, NEG)
            c_out = jnp.einsum('bhgnj,bhjd->bhgnd', jax.nn.softmax(csim, -1), cv)
            imp = csim[..., 1:].mean(axis=2)
            imp = jnp.concatenate([jnp.full(imp.shape[:-1] + (1,), -1000.0, imp.dtype), imp], axis=-1)
            imp = jax.nn.softmax(imp, -1)[..., 1:]
            sel_vals, sel_idx = jax.lax.top_k(imp, NSEL)
            fine_gate_mask = sel_vals > 1e-10
            pos = jnp.arange(n, dtype=jnp.float32)
            rq, rk = (_rope(q, pos), _rope(k, pos))
            nf = n // SBLK
            own = jnp.broadcast_to((jnp.arange(n) // SBLK)[None, None, :, None], (b, KV_HEADS, n, 1))
            idx = jnp.concatenate([sel_idx, own], axis=-1)
            kblocks = rk.reshape(b, KV_HEADS, nf, SBLK, DH)
            vblocks = v.reshape(b, KV_HEADS, nf, SBLK, DH)
            bi = jnp.arange(b)[:, None, None, None]
            hi = jnp.arange(KV_HEADS)[None, :, None, None]
            fk = kblocks[bi, hi, idx].reshape(b, KV_HEADS, n, (NSEL + 1) * SBLK, DH)
            fv = vblocks[bi, hi, idx].reshape(b, KV_HEADS, n, (NSEL + 1) * SBLK, DH)
            sel_m = jnp.repeat(fine_gate_mask[..., None], SBLK, -1).reshape(b, KV_HEADS, n, NSEL * SBLK)
            diag_m = (jnp.arange(n) % SBLK)[:, None] >= jnp.arange(SBLK)[None, :]
            fmask = jnp.concatenate([sel_m, jnp.broadcast_to(diag_m[None, None], (b, KV_HEADS, n, SBLK))], axis=-1)
            fsim = jnp.einsum('bhgnd,bhnjd->bhgnj', rq, fk) * SCALE
            fsim = jnp.where(fmask[:, :, None], fsim, NEG)
            f_out = jnp.einsum('bhgnj,bhnjd->bhgnd', jax.nn.softmax(fsim, -1), fv)
            nwin = n // WIN
            qw = rq.reshape(b, KV_HEADS, G, nwin, WIN, DH)
            kw = rk.reshape(b, KV_HEADS, nwin, WIN, DH)
            vw = v.reshape(b, KV_HEADS, nwin, WIN, DH)
            kcat = jnp.concatenate([jnp.concatenate([jnp.zeros_like(kw[:, :, :1]), kw[:, :, :-1]], 2), kw], 3)
            vcat = jnp.concatenate([jnp.concatenate([jnp.zeros_like(vw[:, :, :1]), vw[:, :, :-1]], 2), vw], 3)
            ssim = jnp.einsum('bhgwid,bhwjd->bhgwij', qw, kcat) * SCALE
            i_, j_ = (jnp.arange(WIN), jnp.arange(2 * WIN))
            delta = i_[:, None] - (j_[None, :] - WIN)
            smask = ((delta >= 0) & (delta <= WIN))[None] & ((jnp.arange(nwin) > 0)[:, None, None] | (j_ >= WIN)[None, None, :])
            ssim = jnp.where(smask[None, None, None], ssim, NEG)
            s_out = jnp.einsum('bhgwij,bhwjd->bhgwid', jax.nn.softmax(ssim, -1), vcat)
            s_out = s_out.reshape(b, KV_HEADS, G, n, DH)
            gates = jax.nn.sigmoid(x @ w_gate + b_gate).reshape(b, n, KV_HEADS, G, 3).transpose(0, 2, 3, 1, 4)
            out = gates[..., 0:1] * c_out + gates[..., 1:2] * f_out + gates[..., 2:3] * s_out
            out = out.transpose(0, 3, 1, 2, 4).reshape(b, n, HEADS * DH)
            return out @ w_out
        key = jax.random.key(seed)
        ks = jax.random.split(key, 16)

        def rnd(i, shape, sc=0.02):
            return jax.random.normal(ks[i], shape, dtype=jnp.float32) * sc
        dim_inner, dim_kv = (HEADS * DH, KV_HEADS * DH)
        return {'hidden_states': jax.random.normal(ks[0], (B, S, DIM), dtype=jnp.float32), 'w_qkv': rnd(1, (DIM, dim_inner + 2 * dim_kv)), 'k_pos': rnd(2, (KV_HEADS, CBLK, DH)), 'v_pos': rnd(3, (KV_HEADS, CBLK, DH)), 'k_cw1': rnd(4, (CDIM, CDIM)), 'k_cb1': jnp.zeros((CDIM,), jnp.float32), 'k_cw2': rnd(5, (CDIM, DH)), 'k_cb2': jnp.zeros((DH,), jnp.float32), 'v_cw1': rnd(6, (CDIM, CDIM)), 'v_cb1': jnp.zeros((CDIM,), jnp.float32), 'v_cw2': rnd(7, (CDIM, DH)), 'v_cb2': jnp.zeros((DH,), jnp.float32), 'mem_ck': rnd(8, (KV_HEADS, 1, DH)), 'mem_cv': rnd(9, (KV_HEADS, 1, DH)), 'w_gate': rnd(10, (DIM, 3 * HEADS)), 'b_gate': jnp.tile(jnp.array([-2.0, -2.0, 2.0], jnp.float32), HEADS), 'w_out': rnd(11, (dim_inner, DIM))}
    _L0_attn_in = _L0_attn_setup()

    def _L0_ffn_setup():
        import jax, jax.numpy as jnp
        import numpy as np
        B, S, H, I, E, K = (4, 512, 256, 128, 32, 4)
        key = jax.random.key(seed)
        k1, k2, k3, k4, k5, k6 = jax.random.split(key, 6)
        hidden_states = jax.random.normal(k1, (B, S, H), dtype=jnp.float32)
        topk_idx = jax.random.randint(k2, (B * S, K), 0, E)
        w = jax.random.uniform(k3, (B * S, K), dtype=jnp.float32)
        topk_weight = w / jnp.sum(w, axis=-1, keepdims=True)
        scale = 0.02
        gate_weight = jax.random.normal(k4, (E, I, H), dtype=jnp.float32) * scale
        up_weight = jax.random.normal(k5, (E, I, H), dtype=jnp.float32) * scale
        down_weight = jax.random.normal(k6, (E, H, I), dtype=jnp.float32) * scale
        return {'hidden_states': hidden_states, 'gate_weight': gate_weight, 'up_weight': up_weight, 'down_weight': down_weight, 'topk_idx': topk_idx, 'topk_weight': topk_weight}
    _L0_ffn_in = _L0_ffn_setup()
    _L0_c = _w((lambda *s: np.random.randn(*s).astype(np.float32) * 0.05)(8, 256))
    _L0_wmod = _w((lambda *s: np.random.randn(*s).astype(np.float32) * 0.05)(256, 6 * 256) * 256 ** (-0.5))

    def _L1_attn_setup():
        import jax, jax.numpy as jnp
        import numpy as np
        EMBED_DIM = 256
        NUM_HEADS = 16
        HEAD_DIM = EMBED_DIM // NUM_HEADS
        D_K = 128
        SCALE = 1.0 / float(np.sqrt(HEAD_DIM))
        LAYER_DEPTH = 6 / 12
        BATCH, SEQ = (2, 256)
        key = jax.random.key(seed)
        ks = jax.random.split(key, 8)
        return {'hidden_states': jax.random.normal(ks[0], (BATCH, SEQ, EMBED_DIM), jnp.float32), 'c_attn_w': jax.random.normal(ks[1], (EMBED_DIM, 3 * EMBED_DIM), jnp.float32) * 0.02, 'c_attn_b': jax.random.normal(ks[2], (3 * EMBED_DIM,), jnp.float32) * 0.02, 'c_proj_w': jax.random.normal(ks[3], (EMBED_DIM, EMBED_DIM), jnp.float32) * 0.02, 'c_proj_b': jax.random.normal(ks[4], (EMBED_DIM,), jnp.float32) * 0.02, 'cam_gate': jax.random.normal(ks[5], (D_K,), jnp.float32) * 0.1, 'cam_w0': jax.random.normal(ks[6], (1,), jnp.float32), 'cam_w1': jax.random.normal(ks[7], (1,), jnp.float32)}
    _L1_attn_in = _L1_attn_setup()

    def _L1_ffn_setup():
        import jax, jax.numpy as jnp
        import numpy as np
        EPS = 1e-05
        ROPE_BASE = 150000.0
        NHEADS = 32
        KVHEADS = 8
        HEAD_DIM = 64
        TOP_K = 4

        def _rms(x, w):
            return x * jax.lax.rsqrt(jnp.mean(x * x, -1, keepdims=True) + EPS) * w

        def _rope(q, k):
            S, hd = (q.shape[1], q.shape[-1])
            half = hd // 2
            inv = 1.0 / ROPE_BASE ** (jnp.arange(half, dtype=jnp.float32) / half)
            ang = jnp.arange(S, dtype=jnp.float32)[:, None] * inv
            cos = jnp.concatenate([jnp.cos(ang), jnp.cos(ang)], -1)[None, :, None, :]
            sin = jnp.concatenate([jnp.sin(ang), jnp.sin(ang)], -1)[None, :, None, :]

            def rot(t):
                t1, t2 = (t[..., :half], t[..., half:])
                return jnp.concatenate([-t2, t1], -1)
            return (q * cos + rot(q) * sin, k * cos + rot(k) * sin)
        key = jax.random.key(seed)
        ks = jax.random.split(key, 12)
        B, S, D, H, E = (1, 128, 256, 256, 16)
        s = 0.02
        return {'x': jax.random.normal(ks[0], (B, S, D), jnp.float32), 'ln_w': jnp.ones((D,), jnp.float32), 'ff_ln_w': jnp.ones((D,), jnp.float32), 'wq': jax.random.normal(ks[1], (D, NHEADS * HEAD_DIM), jnp.float32) * s, 'wk': jax.random.normal(ks[2], (D, KVHEADS * HEAD_DIM), jnp.float32) * s, 'wv': jax.random.normal(ks[3], (D, KVHEADS * HEAD_DIM), jnp.float32) * s, 'wo': jax.random.normal(ks[4], (NHEADS * HEAD_DIM, D), jnp.float32) * s, 'wg': jax.random.normal(ks[5], (D, E), jnp.float32) * s, 'w1': jax.random.normal(ks[6], (E, D, H), jnp.float32) * s, 'w3': jax.random.normal(ks[7], (E, D, H), jnp.float32) * s, 'w2': jax.random.normal(ks[8], (E, H, D), jnp.float32) * s}
    _L1_ffn_in = _L1_ffn_setup()
    _L1_c = _w((lambda *s: np.random.randn(*s).astype(np.float32) * 0.05)(8, 256))
    _L1_wmod = _w((lambda *s: np.random.randn(*s).astype(np.float32) * 0.05)(256, 6 * 256) * 256 ** (-0.5))
    _d = {'L0_attn_hidden_states': _L0_attn_in['hidden_states'], 'L0_attn_w_qkv': _L0_attn_in['w_qkv'], 'L0_attn_k_pos': _L0_attn_in['k_pos'], 'L0_attn_v_pos': _L0_attn_in['v_pos'], 'L0_attn_k_cw1': _L0_attn_in['k_cw1'], 'L0_attn_k_cb1': _L0_attn_in['k_cb1'], 'L0_attn_k_cw2': _L0_attn_in['k_cw2'], 'L0_attn_k_cb2': _L0_attn_in['k_cb2'], 'L0_attn_v_cw1': _L0_attn_in['v_cw1'], 'L0_attn_v_cb1': _L0_attn_in['v_cb1'], 'L0_attn_v_cw2': _L0_attn_in['v_cw2'], 'L0_attn_v_cb2': _L0_attn_in['v_cb2'], 'L0_attn_mem_ck': _L0_attn_in['mem_ck'], 'L0_attn_mem_cv': _L0_attn_in['mem_cv'], 'L0_attn_w_gate': _L0_attn_in['w_gate'], 'L0_attn_b_gate': _L0_attn_in['b_gate'], 'L0_attn_w_out': _L0_attn_in['w_out'], 'L0_ffn_gate_weight': _L0_ffn_in['gate_weight'], 'L0_ffn_up_weight': _L0_ffn_in['up_weight'], 'L0_ffn_down_weight': _L0_ffn_in['down_weight'], 'L0_ffn_topk_idx': _L0_ffn_in['topk_idx'], 'L0_ffn_topk_weight': _L0_ffn_in['topk_weight'], 'L0_c': _L0_c, 'L0_wmod': _L0_wmod, 'L1_attn_c_attn_w': _L1_attn_in['c_attn_w'], 'L1_attn_c_attn_b': _L1_attn_in['c_attn_b'], 'L1_attn_c_proj_w': _L1_attn_in['c_proj_w'], 'L1_attn_c_proj_b': _L1_attn_in['c_proj_b'], 'L1_attn_cam_gate': _L1_attn_in['cam_gate'], 'L1_attn_cam_w0': _L1_attn_in['cam_w0'], 'L1_attn_cam_w1': _L1_attn_in['cam_w1'], 'L1_ffn_ln_w': _L1_ffn_in['ln_w'], 'L1_ffn_ff_ln_w': _L1_ffn_in['ff_ln_w'], 'L1_ffn_wq': _L1_ffn_in['wq'], 'L1_ffn_wk': _L1_ffn_in['wk'], 'L1_ffn_wv': _L1_ffn_in['wv'], 'L1_ffn_wo': _L1_ffn_in['wo'], 'L1_ffn_wg': _L1_ffn_in['wg'], 'L1_ffn_w1': _L1_ffn_in['w1'], 'L1_ffn_w3': _L1_ffn_in['w3'], 'L1_ffn_w2': _L1_ffn_in['w2'], 'L1_c': _L1_c, 'L1_wmod': _L1_wmod}
    _x0 = _d['L0_attn_hidden_states']
    _d['L0_attn_hidden_states'] = jax.random.normal(jax.random.fold_in(jax.random.key(seed), 1), (8, 512, 256), dtype=_x0.dtype)
    del _x0
    return _d

def reference(L0_attn_hidden_states, L0_attn_w_qkv, L0_attn_k_pos, L0_attn_v_pos, L0_attn_k_cw1, L0_attn_k_cb1, L0_attn_k_cw2, L0_attn_k_cb2, L0_attn_v_cw1, L0_attn_v_cb1, L0_attn_v_cw2, L0_attn_v_cb2, L0_attn_mem_ck, L0_attn_mem_cv, L0_attn_w_gate, L0_attn_b_gate, L0_attn_w_out, L0_ffn_gate_weight, L0_ffn_up_weight, L0_ffn_down_weight, L0_ffn_topk_idx, L0_ffn_topk_weight, L0_c, L0_wmod, L1_attn_c_attn_w, L1_attn_c_attn_b, L1_attn_c_proj_w, L1_attn_c_proj_b, L1_attn_cam_gate, L1_attn_cam_w0, L1_attn_cam_w1, L1_ffn_ln_w, L1_ffn_ff_ln_w, L1_ffn_wq, L1_ffn_wk, L1_ffn_wv, L1_ffn_wo, L1_ffn_wg, L1_ffn_w1, L1_ffn_w3, L1_ffn_w2, L1_c, L1_wmod):

    def _L0_attn_ref(hidden_states, w_qkv, k_pos, v_pos, k_cw1, k_cb1, k_cw2, k_cb2, v_cw1, v_cb1, v_cw2, v_cb2, mem_ck, mem_cv, w_gate, b_gate, w_out):
        import jax, jax.numpy as jnp
        import numpy as np
        B, S, DIM = (1, 256, 256)
        HEADS, KV_HEADS = (32, 8)
        DH = DIM // HEADS
        G = HEADS // KV_HEADS
        CBLK = 16
        SBLK = 16
        NSEL = 8
        WIN = 64
        SCALE = DH ** (-0.5)
        NEG = -1e+30
        CDIM = CBLK * DH

        def _rope(x, pos):
            d = x.shape[-1]
            inv = 1.0 / 10000.0 ** (jnp.arange(0, d, 2, dtype=jnp.float32) / d)
            ang = pos[:, None] * inv[None, :]
            cos, sin = (jnp.cos(ang), jnp.sin(ang))
            x1, x2 = (x[..., 0::2], x[..., 1::2])
            return jnp.stack([x1 * cos - x2 * sin, x1 * sin + x2 * cos], axis=-1).reshape(x.shape)

        def _forward(x, w_qkv, k_pos, v_pos, k_cw1, k_cb1, k_cw2, k_cb2, v_cw1, v_cb1, v_cw2, v_cb2, mem_ck, mem_cv, w_gate, b_gate, w_out):
            b, n, _ = x.shape
            di, dkv = (HEADS * DH, KV_HEADS * DH)
            qkv = x @ w_qkv
            q = qkv[..., :di].reshape(b, n, KV_HEADS, G, DH).transpose(0, 2, 3, 1, 4)
            k = qkv[..., di:di + dkv].reshape(b, n, KV_HEADS, DH).transpose(0, 2, 1, 3)
            v = qkv[..., di + dkv:].reshape(b, n, KV_HEADS, DH).transpose(0, 2, 1, 3)
            nc = n // CBLK
            kb = k[:, :, :nc * CBLK].reshape(b, KV_HEADS, nc, CBLK, DH) + k_pos[None, :, None]
            vb = v[:, :, :nc * CBLK].reshape(b, KV_HEADS, nc, CBLK, DH) + v_pos[None, :, None]
            ck = jax.nn.relu(kb.reshape(b, KV_HEADS, nc, CDIM) @ k_cw1 + k_cb1) @ k_cw2 + k_cb2
            cv = jax.nn.relu(vb.reshape(b, KV_HEADS, nc, CDIM) @ v_cw1 + v_cb1) @ v_cw2 + v_cb2
            ck = jnp.concatenate([jnp.broadcast_to(mem_ck[None], (b, KV_HEADS, 1, DH)), ck], axis=2)
            cv = jnp.concatenate([jnp.broadcast_to(mem_cv[None], (b, KV_HEADS, 1, DH)), cv], axis=2)
            csim = jnp.einsum('bhgnd,bhjd->bhgnj', q, ck) * SCALE
            ck_last = jnp.concatenate([jnp.array([-1]), (jnp.arange(nc) + 1) * CBLK - 1])
            cmask = ck_last[None, :] < jnp.arange(n)[:, None]
            csim = jnp.where(cmask, csim, NEG)
            c_out = jnp.einsum('bhgnj,bhjd->bhgnd', jax.nn.softmax(csim, -1), cv)
            imp = csim[..., 1:].mean(axis=2)
            imp = jnp.concatenate([jnp.full(imp.shape[:-1] + (1,), -1000.0, imp.dtype), imp], axis=-1)
            imp = jax.nn.softmax(imp, -1)[..., 1:]
            sel_vals, sel_idx = jax.lax.top_k(imp, NSEL)
            fine_gate_mask = sel_vals > 1e-10
            pos = jnp.arange(n, dtype=jnp.float32)
            rq, rk = (_rope(q, pos), _rope(k, pos))
            nf = n // SBLK
            own = jnp.broadcast_to((jnp.arange(n) // SBLK)[None, None, :, None], (b, KV_HEADS, n, 1))
            idx = jnp.concatenate([sel_idx, own], axis=-1)
            kblocks = rk.reshape(b, KV_HEADS, nf, SBLK, DH)
            vblocks = v.reshape(b, KV_HEADS, nf, SBLK, DH)
            bi = jnp.arange(b)[:, None, None, None]
            hi = jnp.arange(KV_HEADS)[None, :, None, None]
            fk = kblocks[bi, hi, idx].reshape(b, KV_HEADS, n, (NSEL + 1) * SBLK, DH)
            fv = vblocks[bi, hi, idx].reshape(b, KV_HEADS, n, (NSEL + 1) * SBLK, DH)
            sel_m = jnp.repeat(fine_gate_mask[..., None], SBLK, -1).reshape(b, KV_HEADS, n, NSEL * SBLK)
            diag_m = (jnp.arange(n) % SBLK)[:, None] >= jnp.arange(SBLK)[None, :]
            fmask = jnp.concatenate([sel_m, jnp.broadcast_to(diag_m[None, None], (b, KV_HEADS, n, SBLK))], axis=-1)
            fsim = jnp.einsum('bhgnd,bhnjd->bhgnj', rq, fk) * SCALE
            fsim = jnp.where(fmask[:, :, None], fsim, NEG)
            f_out = jnp.einsum('bhgnj,bhnjd->bhgnd', jax.nn.softmax(fsim, -1), fv)
            nwin = n // WIN
            qw = rq.reshape(b, KV_HEADS, G, nwin, WIN, DH)
            kw = rk.reshape(b, KV_HEADS, nwin, WIN, DH)
            vw = v.reshape(b, KV_HEADS, nwin, WIN, DH)
            kcat = jnp.concatenate([jnp.concatenate([jnp.zeros_like(kw[:, :, :1]), kw[:, :, :-1]], 2), kw], 3)
            vcat = jnp.concatenate([jnp.concatenate([jnp.zeros_like(vw[:, :, :1]), vw[:, :, :-1]], 2), vw], 3)
            ssim = jnp.einsum('bhgwid,bhwjd->bhgwij', qw, kcat) * SCALE
            i_, j_ = (jnp.arange(WIN), jnp.arange(2 * WIN))
            delta = i_[:, None] - (j_[None, :] - WIN)
            smask = ((delta >= 0) & (delta <= WIN))[None] & ((jnp.arange(nwin) > 0)[:, None, None] | (j_ >= WIN)[None, None, :])
            ssim = jnp.where(smask[None, None, None], ssim, NEG)
            s_out = jnp.einsum('bhgwij,bhwjd->bhgwid', jax.nn.softmax(ssim, -1), vcat)
            s_out = s_out.reshape(b, KV_HEADS, G, n, DH)
            gates = jax.nn.sigmoid(x @ w_gate + b_gate).reshape(b, n, KV_HEADS, G, 3).transpose(0, 2, 3, 1, 4)
            out = gates[..., 0:1] * c_out + gates[..., 1:2] * f_out + gates[..., 2:3] * s_out
            out = out.transpose(0, 3, 1, 2, 4).reshape(b, n, HEADS * DH)
            return out @ w_out
        return _forward(hidden_states, w_qkv, k_pos, v_pos, k_cw1, k_cb1, k_cw2, k_cb2, v_cw1, v_cb1, v_cw2, v_cb2, mem_ck, mem_cv, w_gate, b_gate, w_out)

    def _L0_ffn_ref(hidden_states, gate_weight, up_weight, down_weight, topk_idx, topk_weight):
        import jax, jax.numpy as jnp
        import numpy as np
        B, S, H, I, E, K = (4, 512, 256, 128, 32, 4)
        b, s, h = hidden_states.shape
        n_experts = gate_weight.shape[0]
        top_k = topk_idx.shape[-1]
        x = hidden_states.reshape(-1, h)
        n = x.shape[0]
        flat_expert = topk_idx.reshape(-1)
        flat_weight = topk_weight.reshape(-1)
        perm = jnp.argsort(flat_expert)
        tok_sorted = jnp.repeat(jnp.arange(n), top_k)[perm]
        group_sizes = jnp.bincount(flat_expert, length=n_experts).astype(jnp.int32)
        xs = x[tok_sorted]
        g = jax.lax.ragged_dot(xs, jnp.swapaxes(gate_weight, 1, 2), group_sizes)
        u = jax.lax.ragged_dot(xs, jnp.swapaxes(up_weight, 1, 2), group_sizes)
        hmid = jax.nn.silu(g) * u
        o = jax.lax.ragged_dot(hmid, jnp.swapaxes(down_weight, 1, 2), group_sizes)
        o = o * flat_weight[perm][:, None]
        y = jnp.zeros((n, h), dtype=x.dtype).at[tok_sorted].add(o)
        return y.reshape(b, s, h)

    def _L1_attn_ref(hidden_states, c_attn_w, c_attn_b, c_proj_w, c_proj_b, cam_gate, cam_w0, cam_w1):
        import jax, jax.numpy as jnp
        import numpy as np
        EMBED_DIM = 256
        NUM_HEADS = 16
        HEAD_DIM = EMBED_DIM // NUM_HEADS
        D_K = 128
        SCALE = 1.0 / float(np.sqrt(HEAD_DIM))
        LAYER_DEPTH = 6 / 12
        BATCH, SEQ = (2, 256)
        qkv = hidden_states @ c_attn_w + c_attn_b
        Q, K, V = jnp.split(qkv, 3, axis=2)
        attn_scores = jnp.einsum('bse,bte->bst', Q, K) * SCALE
        Q_cam, K_cam, V_cam = (Q[:, :, :D_K], K[:, :, :D_K], V[:, :, :D_K])
        base_A = jax.lax.stop_gradient(jax.nn.softmax(jnp.einsum('bsd,btd->bst', Q_cam, K_cam) * SCALE, axis=-1))
        layer_weight = jax.nn.sigmoid(cam_w0[0] + cam_w1[0] * LAYER_DEPTH)
        cam_ctx = jnp.einsum('bst,btd->bsd', base_A, V_cam)
        cam_bias = jnp.einsum('bsd,btd->bst', jnp.tanh(cam_ctx * cam_gate), K_cam)
        cam_bias = cam_bias * (SCALE * layer_weight)
        final_attn = jax.nn.softmax(attn_scores + cam_bias, axis=-1)
        context = jnp.einsum('bst,bte->bse', final_attn, V)
        output = context @ c_proj_w + c_proj_b
        return output

    def _L1_ffn_ref(x, ln_w, ff_ln_w, wq, wk, wv, wo, wg, w1, w3, w2):
        import jax, jax.numpy as jnp
        import numpy as np
        EPS = 1e-05
        ROPE_BASE = 150000.0
        NHEADS = 32
        KVHEADS = 8
        HEAD_DIM = 64
        TOP_K = 4

        def _rms(x, w):
            return x * jax.lax.rsqrt(jnp.mean(x * x, -1, keepdims=True) + EPS) * w

        def _rope(q, k):
            S, hd = (q.shape[1], q.shape[-1])
            half = hd // 2
            inv = 1.0 / ROPE_BASE ** (jnp.arange(half, dtype=jnp.float32) / half)
            ang = jnp.arange(S, dtype=jnp.float32)[:, None] * inv
            cos = jnp.concatenate([jnp.cos(ang), jnp.cos(ang)], -1)[None, :, None, :]
            sin = jnp.concatenate([jnp.sin(ang), jnp.sin(ang)], -1)[None, :, None, :]

            def rot(t):
                t1, t2 = (t[..., :half], t[..., half:])
                return jnp.concatenate([-t2, t1], -1)
            return (q * cos + rot(q) * sin, k * cos + rot(k) * sin)
        B, S, D = x.shape
        h = _rms(x, ln_w)
        q = (h @ wq).reshape(B, S, NHEADS, HEAD_DIM)
        k = (h @ wk).reshape(B, S, KVHEADS, HEAD_DIM)
        v = (h @ wv).reshape(B, S, KVHEADS, HEAD_DIM)
        q, k = _rope(q, k)
        g = NHEADS // KVHEADS
        k = jnp.repeat(k, g, axis=2)
        v = jnp.repeat(v, g, axis=2)
        scores = jnp.einsum('bqhd,bkhd->bhqk', q, k) / np.float32(np.sqrt(HEAD_DIM))
        causal = jnp.tril(jnp.ones((S, S), bool))
        scores = jnp.where(causal[None, None], scores, jnp.float32(-1e+30))
        attn = jax.nn.softmax(scores, -1)
        o = jnp.einsum('bhqk,bkhd->bqhd', attn, v).reshape(B, S, NHEADS * HEAD_DIM)
        x = x + o @ wo
        h = _rms(x, ff_ln_w)
        logits = h @ wg
        topv, topi = jax.lax.top_k(logits, TOP_K)
        gate = jax.nn.softmax(topv, -1)
        bidx = jnp.arange(B)[:, None, None]
        sidx = jnp.arange(S)[None, :, None]
        weights = jnp.zeros_like(logits).at[bidx, sidx, topi].set(gate)
        a = jax.nn.silu(jnp.einsum('bsd,edh->bseh', h, w1)) * jnp.einsum('bsd,edh->bseh', h, w3)
        y = jnp.einsum('bseh,ehd->bsed', a, w2)
        moe = jnp.einsum('bsed,bse->bsd', y, weights)
        return x + moe
    x = L0_attn_hidden_states
    mod = (_silu(L0_c) @ L0_wmod).reshape(L0_c.shape[0], 6, 1, -1)
    sa, ca, ga, sb, cb, gb = (mod[:, 0], mod[:, 1], mod[:, 2], mod[:, 3], mod[:, 4], mod[:, 5])
    ga = (2 * (ga >= 0) - 1) * jnp.maximum(jnp.abs(ga), 0.25)
    gb = (2 * (gb >= 0) - 1) * jnp.maximum(jnp.abs(gb), 0.25)
    h = _layernorm(x, axis=-1) * (1 + ca) + sa
    x = x + ga * _L0_attn_ref(h, L0_attn_w_qkv, L0_attn_k_pos, L0_attn_v_pos, L0_attn_k_cw1, L0_attn_k_cb1, L0_attn_k_cw2, L0_attn_k_cb2, L0_attn_v_cw1, L0_attn_v_cb1, L0_attn_v_cw2, L0_attn_v_cb2, L0_attn_mem_ck, L0_attn_mem_cv, L0_attn_w_gate, L0_attn_b_gate, L0_attn_w_out)
    h = _layernorm(x, axis=-1) * (1 + cb) + sb
    x = x + gb * _L0_ffn_ref(h, L0_ffn_gate_weight, L0_ffn_up_weight, L0_ffn_down_weight, L0_ffn_topk_idx, L0_ffn_topk_weight)
    mod = (_silu(L1_c) @ L1_wmod).reshape(L1_c.shape[0], 6, 1, -1)
    sa, ca, ga, sb, cb, gb = (mod[:, 0], mod[:, 1], mod[:, 2], mod[:, 3], mod[:, 4], mod[:, 5])
    ga = (2 * (ga >= 0) - 1) * jnp.maximum(jnp.abs(ga), 0.25)
    gb = (2 * (gb >= 0) - 1) * jnp.maximum(jnp.abs(gb), 0.25)
    h = _layernorm(x, axis=-1) * (1 + ca) + sa
    x = x + ga * _L1_attn_ref(h, L1_attn_c_attn_w, L1_attn_c_attn_b, L1_attn_c_proj_w, L1_attn_c_proj_b, L1_attn_cam_gate, L1_attn_cam_w0, L1_attn_cam_w1)
    h = _layernorm(x, axis=-1) * (1 + cb) + sb
    x = x + gb * _L1_ffn_ref(h, L1_ffn_ln_w, L1_ffn_ff_ln_w, L1_ffn_wq, L1_ffn_wk, L1_ffn_wv, L1_ffn_wo, L1_ffn_wg, L1_ffn_w1, L1_ffn_w3, L1_ffn_w2)
    return x

_drawn_inputs = setup_inputs


def setup_inputs(seed=0):
    import zlib

    import numpy as np

    out = dict(_drawn_inputs(seed))
    spreads = {'L0_attn_k_cb1': (0.0, 0.8),
     'L0_attn_k_cb2': (0.0, 0.8),
     'L0_attn_v_cb1': (0.0, 0.8),
     'L0_attn_v_cb2': (0.0, 0.8),
     'L1_ffn_ln_w': (1.0, 0.6),
     'L1_ffn_ff_ln_w': (1.0, 0.6)}
    factors = {'L0_attn_w_qkv': 8.0,
     'L0_attn_k_pos': 8.0,
     'L0_attn_v_pos': 8.0,
     'L0_attn_k_cw1': 8.0,
     'L0_attn_k_cw2': 8.0,
     'L0_attn_v_cw1': 8.0,
     'L0_attn_v_cw2': 8.0,
     'L0_attn_mem_ck': 8.0,
     'L0_attn_mem_cv': 8.0,
     'L0_attn_w_gate': 8.0,
     'L0_attn_w_out': 8.0,
     'L0_ffn_gate_weight': 8.0,
     'L0_ffn_up_weight': 8.0,
     'L0_ffn_down_weight': 8.0,
     'L0_ffn_topk_weight': 8.0,
     'L0_c': 8.0,
     'L0_wmod': 8.0,
     'L1_attn_c_attn_w': 8.0,
     'L1_attn_c_attn_b': 8.0,
     'L1_attn_c_proj_w': 8.0,
     'L1_attn_c_proj_b': 8.0,
     'L1_attn_cam_gate': 8.0,
     'L1_ffn_wq': 8.0,
     'L1_ffn_wk': 8.0,
     'L1_ffn_wv': 6.78,
     'L1_ffn_wo': 6.868,
     'L1_ffn_wg': 8.0,
     'L1_ffn_w1': 8.0,
     'L1_ffn_w3': 8.0,
     'L1_ffn_w2': 8.0}
    for name, (base, spread) in spreads.items():
        noise = np.random.default_rng([zlib.crc32(name.encode()), seed]).standard_normal(out[name].shape)
        drawn = base * np.exp(spread * noise) if base else spread * noise
        out[name] = jnp.asarray(drawn.astype(out[name].dtype))
    for name, factor in factors.items():
        out[name] = (out[name] * factor).astype(out[name].dtype)
    return out
```

```python
import math
from contextlib import ExitStack

import numpy as np
import concourse.bass as bass
from concourse import mybir

F32 = mybir.dt.float32
U32 = mybir.dt.uint32
I32 = mybir.dt.int32
ALU = mybir.AluOpType
ACT = mybir.ActivationFunctionType
AX = mybir.AxisListType.X
NEG = -1e30
BIG = 3.0e38
EPS = 1e-5
S0 = 8 ** -0.5
S1 = 0.25
S2 = 0.125


def flat(ws):
    for w in ws:
        if w is None:
            continue
        if isinstance(w, list):
            yield from flat(w)
        else:
            yield w


class Queue:

    def __init__(self, eng, sem, chained=False):
        self.eng, self.sem, self.n, self.seen, self.chained = eng, sem, 0, {}, chained

    def wait(self, *marks):
        for sem, v in flat(marks):
            if self.seen.get(sem, 0) < v:
                self.seen[sem] = v
                self.eng.wait_ge(sem, v)

    def __call__(self, fn, *marks):
        if self.chained:
            self.wait(self.mark())
        self.wait(*marks)
        self.n += 1
        fn(self.eng).then_inc(self.sem, 1)
        return self.mark()

    def mark(self):
        return (self.sem, self.n)

    def dma(self, out, in_, count, *marks):
        self.wait(*marks)
        count.n += 16
        self.eng.dma_start(out, in_).then_inc(count.sem, 16)
        return (count.sem, count.n)


class Count:
    def __init__(self, sem):
        self.sem, self.n = sem, 0

    def mark(self):
        return (self.sem, self.n)


class Ring:

    def __init__(self, bufs):
        self.bufs, self.free, self.k = bufs, [None] * len(bufs), 0

    def take(self):
        i = self.k % len(self.bufs)
        self.k += 1
        return i, self.bufs[i], self.free[i]


def consts():
    c = {}
    c["ident"] = np.eye(128, dtype=np.float32)
    pos = np.arange(512, dtype=np.float32)
    inv = (1.0 / 10000.0 ** (np.arange(0, 8, 2, dtype=np.float32) / 8)).astype(np.float32)
    ang = (pos[:, None] * inv[None, :]).astype(np.float32)
    cos, sin = np.cos(ang).astype(np.float32), np.sin(ang).astype(np.float32)
    csq = np.zeros((128, 512), np.float32)
    cok = np.zeros((128, 512), np.float32)
    sik = np.zeros((128, 512), np.float32)
    for g in range(4):
        for d in range(8):
            sg = -1.0 if d % 2 == 0 else 1.0
            csq[32 * g + d] = cos[:, d // 2]
            csq[32 * g + 8 + d] = sg * sin[:, d // 2]
            csq[32 * g + 16 + d] = 1.0
            for o in (0, 8):
                cok[32 * g + o + d] = cos[:, d // 2]
                sik[32 * g + o + d] = sg * sin[:, d // 2]
    c["rot0"] = np.stack([csq, cok, sik], 1)
    inv = (1.0 / 150000.0 ** (np.arange(32, dtype=np.float32) / 32)).astype(np.float32)
    ang = (pos[:, None] * inv[None, :]).astype(np.float32)
    cos, sin = np.cos(ang).astype(np.float32), np.sin(ang).astype(np.float32)
    csq = np.zeros((128, 512), np.float32)
    cok = np.zeros((128, 512), np.float32)
    sik = np.zeros((128, 512), np.float32)
    for d in range(64):
        sg = -1.0 if d < 32 else 1.0
        csq[d] = cos[:, d % 32]
        csq[64 + d] = sg * sin[:, d % 32]
        for o in (0, 64):
            cok[o + d] = cos[:, d % 32]
            sik[o + d] = sg * sin[:, d % 32]
    c["rot1"] = np.stack([csq, cok, sik], 1)
    p = np.arange(128)
    own = np.ones((128, 512), np.float32)
    k = np.arange(128)
    own[:, 384:] = np.where((k[None] // 16 == p[:, None] // 16) & (k[None] <= p[:, None]), 0.0, 1.0)
    c["own"] = own
    k = np.arange(256)
    dl = 128 + p[:, None] - k[None]
    c["slide"] = np.where((dl >= 0) & (dl <= 64), 0.0, NEG).astype(np.float32)
    causal = np.zeros((128, 512), np.float32)
    causal[:, 384:] = np.where(np.arange(128)[None] <= p[:, None], 0.0, NEG)
    c["causal"] = causal
    mc = np.zeros((128, 4, 33), np.float32)
    last = np.concatenate([[-1], (np.arange(32) + 1) * 16 - 1])
    for i in range(4):
        mc[:, i] = np.where(last[None] < (128 * i + p)[:, None], 0.0, NEG)
    c["maskc"] = mc
    c["iota"] = np.tile(np.arange(32, dtype=np.float32), (128, 1))
    return c


def program(nc, D, out):
    with ExitStack() as top:
        def sem(n):
            return top.enter_context(nc.semaphore(n))

        def sbt(ctx, n, shape, dt=F32):
            return ctx.enter_context(nc.sbuf_tensor(n, shape, dt))

        V = Queue(nc.vector, sem("s_vec"), True)
        G = Queue(nc.gpsimd, sem("s_pool"), True)
        A = Queue(nc.scalar, sem("s_act"))
        T = Queue(nc.tensor, sem("s_pe"))
        SP = Queue(nc.sync, sem("s_sp"))
        c_w = Count(sem("c_w"))
        c_c = Count(sem("c_c"))
        c_x = Count(sem("c_x"))
        c_xa = [Count(sem(f"c_xa{i}")) for i in range(2)]
        c_k = Count(sem("c_k"))
        c_e = [Count(sem(f"c_e{i}")) for i in range(3)]
        c_o = Count(sem("c_o"))

        def fence():
            marks = [q.mark() for q in (V, G, A, T)] + [c.mark() for c in (c_c, c_w, c_x, c_k, c_o, *c_e, *c_xa)]
            for q in (V, G, A, T, SP):
                q.wait(marks)

        PS = top.enter_context(nc.psum_tensor("PS", [128, 8, 512], F32))
        ident = sbt(top, "ident", [128, 128])
        ones = sbt(top, "ones", [128, 128])
        silu = sbt(top, "silu", [128, 2, 2, 8])
        mb = sbt(top, "mb", [128, 3, 256])
        mtmp = sbt(top, "mtmp", [128, 2, 256])
        cbt = sbt(top, "cbt", [128, 2, 128])
        st6 = sbt(top, "st6", [128, 4, 6])
        mv = sbt(top, "mv", [128, 4, 2])
        rs = sbt(top, "rs", [128, 3, 4])

        xin = D["x"].rearrange("b (i p) d -> p (b i) d", p=128)
        xout = out.rearrange("b (i p) d -> p (b i) d", p=128)
        SP.dma(ident[:], D["ident"], c_c)
        SP.dma(silu[:, 0, :, :], D["c0"], c_c)
        w_c = SP.dma(silu[:, 1, :, :], D["c1"], c_c)
        home = {}

        def X(g):
            return home["at"][:, g % home["n"], :]

        v_ones = V(lambda e: e.memset(ones[:], 1.0))
        sl = silu[:].rearrange("p a b c -> p (a b c)")
        a_silu = A(lambda e: e.activation(sl, sl, ACT.Silu), w_c)

        def mod_rows(layer, b, wmod, wready, ring):
            for k in range(2):
                vb = V(lambda e, k=k: e.tensor_scalar(cbt[:, k, :], ones[:], silu[:, layer, k, b:b + 1], None,
                                                      ALU.mult), a_silu, T.mark())
            i1, p1, f1 = ring.take()
            i2, p2, f2 = ring.take()
            for o, n, p in ((0, 512, p1), (512, 256, p2)):
                for k in range(2):
                    pe = T(lambda e, k=k, o=o, n=n, p=p: e.matmul(
                        p[:, 0:n], cbt[:, k, :], wmod[:, k, o:o + n],
                        start=(k == 0), stop=(k == 1)), vb, wready, f1, f2)
            V(lambda e: e.tensor_copy(mb[:, 0, :], p1[:, 0:256]), pe)
            ring.free[i1] = V(lambda e: e.tensor_scalar(mb[:, 1, :], p1[:, 256:512], 1.0, None, ALU.add))
            V(lambda e: e.tensor_scalar(mtmp[:, 0, :], p2[:, 0:256], 0.0, 2.0, ALU.is_ge, ALU.mult))
            ring.free[i2] = V(lambda e: e.tensor_scalar(mtmp[:, 1, :], p2[:, 0:256], -1.0, None, ALU.mult))
            V(lambda e: e.tensor_tensor(mtmp[:, 1, :], p2[:, 0:256], mtmp[:, 1, :], ALU.max))
            V(lambda e: e.tensor_scalar(mtmp[:, 1, :], mtmp[:, 1, :], 0.25, None, ALU.max))
            v = V(lambda e: e.scalar_tensor_tensor(mb[:, 2, :], mtmp[:, 0, :], -1.0, mtmp[:, 1, :],
                                                   ALU.add, ALU.mult))
            ring.free[i1] = ring.free[i2] = v
            return v

        def layernorm(b, dst, *marks):
            for i in range(4):
                V(lambda e, i=i: e.bn_stats(st6[:, i, :], X(4 * b + i)), home["ready"](b))
                V(lambda e, i=i: e.bn_aggr(mv[:, i, :], st6[:, i, :]))
            v = V(lambda e: e.tensor_scalar(rs[:, 0, :], mv[:, :, 1], EPS, None, ALU.add))
            a = A(lambda e: e.activation(rs[:, 1, :], rs[:, 0, :], ACT.Sqrt), v)
            V(lambda e: e.reciprocal(rs[:, 2, :], rs[:, 1, :]), a)
            for i in range(4):
                V(lambda e, i=i: e.tensor_scalar(dst[:, i, :], X(4 * b + i), mv[:, i, 0:1],
                                                 rs[:, 2, i:i + 1], ALU.subtract, ALU.mult), *marks)
                V(lambda e, i=i: e.tensor_tensor(dst[:, i, :], dst[:, i, :], mb[:, 1, :], ALU.mult))
                v = V(lambda e, i=i: e.tensor_tensor(dst[:, i, :], dst[:, i, :], mb[:, 0, :], ALU.add))
            return v

        def rmsnorm(src, w, dst, sq, *marks):
            for i in range(4):
                V(lambda e, i=i: e.tensor_tensor(sq, src[:, i, :], src[:, i, :], ALU.mult), *marks)
                V(lambda e, i=i: e.tensor_reduce(rs[:, 1, i:i + 1], sq, AX, ALU.add))
            v = V(lambda e: e.tensor_scalar(rs[:, 0, :], rs[:, 1, :], 1.0 / 256, EPS, ALU.mult, ALU.add))
            a = A(lambda e: e.activation(rs[:, 1, :], rs[:, 0, :], ACT.Sqrt), v)
            V(lambda e: e.reciprocal(rs[:, 2, :], rs[:, 1, :]), a)
            for i in range(4):
                v = V(lambda e, i=i: e.scalar_tensor_tensor(dst[:, i, :], src[:, i, :], rs[:, 2, i:i + 1], w,
                                                            ALU.mult, ALU.mult))
            return v

        def to_columns(src, dst, at, ring, ready, *marks):
            for k in range(2):
                n, p, f = ring.take()
                for i in range(4):
                    pe = T(lambda e, i=i, k=k, p=p: e.transpose(
                        p[:, 128 * i:128 * i + 128], src[:, i, 128 * k:128 * k + 128], ident[:]),
                        ready, f, w_c)
                q = (V, A)[k]
                if k == 0:
                    m0 = V(lambda e, k=k, p=p: e.tensor_copy(dst[:, k, at:at + 512], p[:, :]), pe, *marks)
                    ring.free[n] = m0
                else:
                    m1 = A(lambda e, k=k, p=p: e.activation(dst[:, k, at:at + 512], p[:, :], ACT.Copy), pe, *marks)
                    ring.free[n] = m1
            return [m0, m1]

        def add_gated(tile, psum, pe, tmp):
            V(lambda e: e.tensor_tensor(tmp, psum, mb[:, 2, :], ALU.mult), pe)
            return V(lambda e: e.tensor_tensor(X(tile), X(tile), tmp, ALU.add))

        def evac(q, out_, in_, *marks):
            if q is V:
                return V(lambda e: e.tensor_copy(out_, in_), *marks)
            return A(lambda e: e.activation(out_, in_, ACT.Copy), *marks)

        def phase_a(ctx):
            def sb(n, shape, dt=F32):
                return sbt(ctx, "a_" + n, shape, dt)

            wmod = sb("wmod", [128, 2, 768])
            wq = sb("wq", [128, 2, 1024])
            wkA = sb("wkA", [128, 2, 1024])
            wkB = sb("wkB", [128, 2, 1024])
            wkv = sb("wkv", [128, 2, 128])
            wg = sb("wg", [128, 2, 96])
            bg = sb("bg", [1, 96])
            wo = sb("wo", [128, 2, 256])
            cw1 = sb("cw1", [40, 16, 128])
            pos = sb("pos", [40, 16, 8])
            cb1 = sb("cb1", [128, 2])
            cw2k = sb("cw2k", [128, 128])
            cb2k = sb("cb2k", [128, 1])
            cw2v = sb("cw2v", [128, 8])
            cb2v = sb("cb2v", [128, 8])
            mck = sb("mck", [128, 8])
            mcv = sb("mcv", [128, 8, 8])
            rot = sb("rot", [128, 3, 512])
            own = sb("own", [128, 512])
            slide = sb("slide", [128, 256])
            maskc = sb("maskc", [128, 4, 33])
            for t, n in ((wmod, "wmod0a"), (wq, "wq0"), (wkA, "wkA0"), (wkB, "wkB0"), (wkv, "wkv0"), (wg, "wg0"),
                         (bg, "bg0"), (wo, "wo0"), (cb1, "cb1"), (cw2k, "cw2k"),
                         (cb2k, "cb2k"), (cw2v, "cw2v"), (cb2v, "cb2v"), (mck, "mck"), (mcv, "mcv"),
                         (rot, "rot0"), (own, "own"), (slide, "slide"), (maskc, "maskc")):
                w = SP.dma(t[:], D[n], c_w)
            for j in range(2):
                SP.dma(cw1[32 * j:32 * j + 8, :, :], D["cw1"][:, j], c_w)
                w = SP.dma(pos[32 * j:32 * j + 8, :, :], D["kvpos"][:, j], c_w)
            Xa = sb("X", [128, 8, 256])
            home.update(at=Xa, n=8)
            m_xa, x_done = {}, {}

            def load_x(b):
                m_xa[b] = SP.dma(Xa[:, 4 * (b % 2):4 * (b % 2) + 4, :], xin[:, 4 * b:4 * b + 4, :], c_xa[b % 2],
                                 x_done.get(b - 2))

            home["ready"] = lambda b: m_xa[b]
            h = sb("h", [128, 4, 256])
            hT = sb("hT", [128, 2, 512])
            qs = sb("qs", [128, 8, 512])
            ks = sb("ks", [128, 8, 512])
            t1 = sb("t1", [128, 2, 512])
            kv = sb("kv", [128, 512])
            kr = sb("kr", [40, 8, 512])
            vt = sb("vt", [128, 4, 64])
            gt = sb("gt", [128, 4, 96])
            bias1 = sb("bias1", [128, 2, 8])
            hk = sb("hk", [128, 256])
            rv = sb("rv", [128, 8, 4, 32])
            ckt = sb("ckt", [128, 8, 33])
            cvt = sb("cvt", [128, 8, 32])
            cs = sb("cs", [128, 32, 33])
            eC = sb("eC", [128, 32, 32])
            eM = sb("eM", [128, 32])
            z4 = sb("z4", [128, 6, 32])
            im = sb("im", [128, 8, 33])
            im2 = sb("im2", [128, 8, 33])
            imn = sb("imn", [128, 8, 32])
            m8 = sb("m8", [128, 8, 8])
            rp = sb("rp", [128, 8, 32])
            sel = sb("sel", [128, 4, 8, 32])
            eT = sb("eT", [128, 8, 128])
            acc = sb("acc", [128, 4, 256])
            tmp = sb("tmp", [128, 256])
            zf = sb("zf", [128, 2, 64])
            bs = sb("bs", [128, 4, 2])
            fm = sb("fm", [128, 3, 512])
            sm = sb("sm", [128, 3, 256])
            ef = sb("ef", [128, 3, 512])
            es = sb("es", [128, 3, 256])
            tf = sb("tf", [128, 3, 512])
            ts_ = sb("ts", [128, 3, 256])
            mx = sb("mx", [128, 3, 512])
            oT = sb("oT", [128, 2, 128])

            RS = Ring([PS[:, i, :] for i in range(3)])
            RF = Ring([PS[:, 3 + i, :] for i in range(2)])
            RT = Ring([PS[:, 5, 0:256], PS[:, 6, 0:256]])
            RO = Ring([PS[:, 7, :]])

            V(lambda e: e.memset(es[:], 0.0))
            V(lambda e: e.memset(im[:], -4000.0))
            V(lambda e: e.memset(cvt[:], 0.0))
            V(lambda e: e.tensor_scalar(ckt[:, :, 0], mck[:], S0, None, ALU.mult), w)
            for j in range(2):
                n, p, f = RS.take()
                for t in range(16):
                    pe = T(lambda e, t=t, j=j, p=p: e.matmul(p[:, 0:8], cw1[32 * j:32 * j + 8, t, :], pos[32 * j:32 * j + 8, t, :],
                                                             start=(t == 0), stop=(t == 15)), w, f)
                RS.free[n] = V(lambda e, j=j, p=p: e.tensor_scalar(bias1[:, j, :], p[:, 0:8], cb1[:, j:j + 1], None,
                                                                   ALU.add), pe)

            load_x(0)
            for b in range(8):
                if b < 7:
                    load_x(b + 1)
                mod_rows(0, b, wmod, w, RS)
                lv = layernorm(b, h, T.mark())
                hr = to_columns(h, hT, 0, RS, lv, T.mark())
                for hh in range(8):
                    c = slice(128 * hh, 128 * hh + 128)
                    n, p, f = RS.take()
                    for k in range(2):
                        pe = T(lambda e, k=k, c=c, p=p: e.matmul(p[:, :], wq[:, k, c], hT[:, k, :], start=(k == 0),
                                                                 stop=(k == 1)), hr, w, f)
                    RS.free[n] = V(lambda e, hh=hh, p=p: e.tensor_tensor(qs[:, hh, :], p[:, :], rot[:, 0, :],
                                                                         ALU.mult), pe)
                    for j, wk in ((0, wkA), (1, wkB)):
                        n, p, f = RS.take()
                        for k in range(2):
                            pe = T(lambda e, k=k, c=c, p=p, wk=wk: e.matmul(
                                p[:, :], wk[:, k, c], hT[:, k, :], start=(k == 0), stop=(k == 1)), f)
                        v = V(lambda e, j=j, p=p: e.tensor_tensor(t1[:, j, :], p[:, :], rot[:, 1 + j, :],
                                                                  ALU.mult), pe)
                        RS.free[n] = v
                    m_ks = V(lambda e, hh=hh: e.tensor_tensor(ks[:, hh, :], t1[:, 0, :], t1[:, 1, :], ALU.add))
                n, p, f = RS.take()
                for k in range(2):
                    pe = T(lambda e, k=k, p=p: e.matmul(p[:, :], wkv[:, k, :], hT[:, k, :], start=(k == 0),
                                                        stop=(k == 1)), f)
                RS.free[n] = v = V(lambda e, p=p: e.tensor_copy(kv[:], p[:, :]), pe, c_k.mark())
                for j in range(2):
                    for hh in range(8):
                        r = 64 * j + 8 * hh
                        m_kr = SP.dma(kr[32 * j:32 * j + 8, hh, :], kv[r:r + 8, :], c_k, v, T.mark())
                n, p, f = RS.take()
                for i in range(4):
                    for k in range(2):
                        pe = T(lambda e, i=i, k=k, p=p: e.matmul(
                            p[:, 64 * i:64 * i + 64], hT[:, k, 128 * i:128 * i + 128], wkv[:, k, 64:128],
                            start=(k == 0), stop=(k == 1)), f)
                m_vt = RS.free[n] = V(lambda e, p=p: e.tensor_copy(vt[:].rearrange("p a b -> p (a b)"),
                                                                   p[:, 0:256]), pe)
                n, p, f = RS.take()
                for i in range(4):
                    for k in range(2):
                        T(lambda e, i=i, k=k, p=p: e.matmul(
                            p[:, 96 * i:96 * i + 96], hT[:, k, 128 * i:128 * i + 128], wg[:, k, :],
                            start=(k == 0), stop=False), f)
                    pe = T(lambda e, i=i, p=p: e.matmul(p[:, 96 * i:96 * i + 96], ones[0:1, :], bg[0:1, :],
                                                        start=False, stop=True), v_ones)
                m_gt = RS.free[n] = A(lambda e, p=p: e.activation(gt[:].rearrange("p a b -> p (a b)"), p[:, 0:384],
                                                                  ACT.Sigmoid), pe, V.mark())
                for j in range(2):
                    n, p, f = RS.take()
                    for t in range(16):
                        pe = T(lambda e, t=t, j=j, p=p: e.matmul(
                            p[:, 0:256], cw1[32 * j:32 * j + 8, t, :],
                            kr[32 * j:32 * j + 8, :, :].rearrange("d h (c t) -> d h c t", t=16)[:, :, :, t],
                            start=(t == 0), stop=(t == 15)), m_kr, f)
                    V(lambda e, j=j, p=p: e.tensor_tensor(
                        hk[:].rearrange("p (h c) -> p h c", h=8), p[:, 0:256].rearrange("p (h c) -> p h c", h=8),
                        bias1[:, j, :].unsqueeze(2).to_broadcast([128, 8, 32]), ALU.add), pe)
                    if j == 0:
                        v = RS.free[n] = V(lambda e: e.tensor_scalar(hk[:], hk[:], 0.0, None, ALU.max))
                        n, p, f = RS.take()
                        pe = T(lambda e, p=p: e.matmul(p[:, 0:256], cw2k[:], hk[:], start=True, stop=True), v, f)
                        m_ck = RS.free[n] = V(lambda e, p=p: e.tensor_scalar(
                            ckt[:, :, 1:33], p[:, 0:256].rearrange("p (h c) -> p h c", h=8), cb2k[:, 0:1], S0,
                            ALU.add, ALU.mult), pe)
                    else:
                        for g in range(4):
                            v = V(lambda e, g=g: e.tensor_scalar(
                                rv[:, :, g, :], hk[:].rearrange("p (h c) -> p h c", h=8), 0.0, None, ALU.max))
                        RS.free[n] = v
                        n, p, f = RS.take()
                        for hh in range(8):
                            pe = T(lambda e, hh=hh, p=p: e.matmul(
                                p[:, 8 * hh:8 * hh + 8], rv[:, hh, :, :].rearrange("p g c -> p (g c)"), cw2v[:],
                                start=True, stop=True), v, f)
                        for g in range(4):
                            r = slice(32 * g, 32 * g + 32)
                            m_cv = RS.free[n] = V(lambda e: e.tensor_tensor(
                                cvt[r, :, 8 * g:8 * g + 8], p[r, 0:64].rearrange("p (h d) -> p h d", h=8),
                                cb2v[r, :].unsqueeze(1).to_broadcast([32, 8, 8]), ALU.add), pe)
                m_ex = A.mark()
                for i in range(4):
                    qc = slice(128 * i, 128 * i + 128)
                    for g in range(4):
                        n, p, f = RS.take()
                        for hh in range(8):
                            pe = T(lambda e: e.matmul(
                                p[:, 33 * hh:33 * hh + 33], qs[32 * g:32 * g + 32, hh, qc],
                                ckt[32 * g:32 * g + 32, hh, :], start=True, stop=True,
                                tile_position=(32 * g, 0)), m_ck, f)
                        RS.free[n] = V(lambda e: e.tensor_tensor(
                            cs[:].rearrange("p (h g) j -> p h g j", g=4)[:, :, g, :],
                            p[:, 0:264].rearrange("p (u j) -> p u j", u=8),
                            maskc[:, i, :].unsqueeze(1).to_broadcast([128, 8, 33]), ALU.add), pe, m_ex)
                    V(lambda e: e.tensor_reduce(z4[:, 0, :], cs[:], AX, ALU.max))
                    V(lambda e: e.tensor_reduce(im[:, :, 1:33], cs[:].rearrange("p (h g) j -> p h j g", g=4)
                                                [:, :, 1:33, :], AX, ALU.add))
                    v = V(lambda e: e.tensor_tensor(cs[:], cs[:], z4[:, 0, :].unsqueeze(2).to_broadcast([128, 32, 33]),
                                                    ALU.subtract))
                    V(lambda e: e.tensor_reduce(z4[:, 1, 0:8], im[:], AX, ALU.max))
                    v2 = V(lambda e: e.tensor_tensor(im2[:], im[:], z4[:, 1, 0:8].unsqueeze(2)
                                                     .to_broadcast([128, 8, 33]), ALU.subtract))
                    A(lambda e: e.activation(eM[:], cs[:, :, 0], ACT.Exp), v)
                    a = A(lambda e: e.activation(eC[:], cs[:, :, 1:33], ACT.Exp), v, T.mark())
                    m_ex = a
                    a2 = A(lambda e: e.activation(im2[:], im2[:], ACT.Exp, scale=0.25), v2)
                    for half in range(2):
                        n, p, f = RF.take()
                        for u in range(4):
                            hh = 4 * half + u
                            pe = T(lambda e, u=u, hh=hh, p=p: e.transpose(
                                p[:, 128 * u:128 * u + 128],
                                eC[:, 4 * hh:4 * hh + 4, :].rearrange("p g c -> p (g c)"), ident[:]), a, f)
                        a3 = RF.free[n] = A(lambda e, half=half, p=p: e.activation(
                            eT[:, 4 * half:4 * half + 4, :].rearrange("p a b -> p (a b)"), p[:, :], ACT.Copy), pe)
                    n, p, f = RS.take()
                    for hh in range(8):
                        pe = T(lambda e: e.matmul(p[:, 32 * hh:32 * hh + 32], eT[:, hh, :], cvt[:, hh, :],
                                                  start=True, stop=True), a3, m_cv, f)
                    V(lambda e: e.tensor_reduce(z4[:, 2, :], eC[:], AX, ALU.add), a)
                    V(lambda e: e.tensor_tensor(z4[:, 2, :], z4[:, 2, :], eM[:], ALU.add))
                    V(lambda e: e.reciprocal(z4[:, 3, :], z4[:, 2, :]))
                    V(lambda e, i=i: e.tensor_tensor(z4[:, 3, :], z4[:, 3, :], gt[:, i, 0:96:3], ALU.mult), m_gt)
                    ai = acc[:, i, :].rearrange("p (h g d) -> p h g d", h=8, g=4)
                    V(lambda e, ai=ai: e.tensor_tensor(
                        ai, eM[:].rearrange("p (h g) -> p h g", g=4).unsqueeze(3).to_broadcast([128, 8, 4, 8]),
                        mcv[:].unsqueeze(2).to_broadcast([128, 8, 4, 8]), ALU.mult))
                    RS.free[n] = V(lambda e, i=i, p=p: e.tensor_tensor(acc[:, i, :], acc[:, i, :], p[:, 0:256],
                                                                       ALU.add), pe)
                    V(lambda e, i=i: e.tensor_tensor(
                        acc[:, i, :].rearrange("p (a d) -> p a d", d=8),
                        acc[:, i, :].rearrange("p (a d) -> p a d", d=8),
                        z4[:, 3, :].unsqueeze(2).to_broadcast([128, 32, 8]), ALU.mult))
                    V(lambda e: e.tensor_reduce(z4[:, 1, 8:16], im2[:], AX, ALU.add), a2)
                    V(lambda e: e.reciprocal(z4[:, 1, 16:24], z4[:, 1, 8:16]))
                    V(lambda e: e.tensor_tensor(imn[:], im2[:, :, 1:33], z4[:, 1, 16:24].unsqueeze(2)
                                                .to_broadcast([128, 8, 32]), ALU.mult))
                    for hh in range(8):
                        V(lambda e, hh=hh: e.max(m8[:, hh, :], imn[:, hh, :]))
                        V(lambda e, hh=hh: e.match_replace(rp[:, hh, :], m8[:, hh, :], imn[:, hh, :], -1.0))
                    V(lambda e: e.tensor_scalar(rp[:], rp[:], 0.0, NEG, ALU.is_ge, ALU.mult))
                    V(lambda e: e.tensor_scalar(imn[:], imn[:], 1e-10, NEG, ALU.is_le, ALU.mult))
                    m_sel = V(lambda e, i=i: e.tensor_tensor(sel[:, i, :, :], rp[:], imn[:], ALU.min))

                jobs = [(i, hh, g) for i in range(4) for hh in range(8) for g in range(4)]
                N = len(jobs)
                stt = [dict() for _ in jobs]
                m_mx = {}
                mx_free = [None] * 3

                def score(t):
                    i, hh, g = jobs[t]
                    s = stt[t]
                    nk = 128 * (i + 1)
                    if g == 0:
                        r = (t // 4) % 3
                        m_mx[t // 4] = G(lambda e, i=i, hh=hh, r=r, nk=nk: e.tensor_tensor(
                            mx[:, r, 0:nk].rearrange("p (a c) -> p a c", c=16),
                            sel[:, i, hh, 0:nk // 16].unsqueeze(2).to_broadcast([128, nk // 16, 16]),
                            own[:, 512 - nk:512].rearrange("p (a c) -> p a c", c=16), ALU.mult), m_sel, mx_free[r])
                    n, p, f = RS.take()
                    s["pe"] = T(lambda e: e.matmul(p[:, 0:nk], qs[32 * g:32 * g + 32, hh, 128 * i:128 * i + 128],
                                                   ks[32 * g:32 * g + 32, hh, 0:nk], start=True, stop=True,
                                                   tile_position=(32 * g, 0)), m_ks, f)
                    r, w4 = t % 3, t % 4
                    old = stt[t - 3].get("exp") if t >= 3 else A.mark()
                    old4 = stt[t - 4].get("exp") if t >= 4 else None
                    V(lambda e: e.tensor_tensor_reduce(fm[:, r, 0:nk], p[:, 0:nk], mx[:, (t // 4) % 3, 0:nk], -S0, BIG,
                                                       ALU.add, ALU.min, bs[:, w4, 0:1]),
                      s["pe"], m_mx[t // 4], old, old4)
                    lo = 64 if i else 128
                    RS.free[n] = s["v"] = V(lambda e: e.tensor_tensor_reduce(
                        sm[:, r, lo:256], p[:, nk - 256 + lo:nk], slide[:, lo:256], -S0, BIG,
                        ALU.add, ALU.min, bs[:, w4, 1:2]))
                    if g == 3:
                        mx_free[(t // 4) % 3] = s["v"]
                    c = 4 * hh + g
                    told = stt[t - 3].get("tr") if t >= 3 else T.mark()
                    if t >= 64:
                        zold = zfree.get(i % 2)
                    else:
                        zold = V.mark()
                    A(lambda e: e.activation(ef[:, r, 0:nk], fm[:, r, 0:nk], ACT.Exp, bias=bs[:, w4, 0:1], scale=-1.0,
                                             accum_out=zf[:, i % 2, c:c + 1]), s["v"], told, zold)
                    s["exp"] = A(lambda e: e.activation(es[:, r, lo:256], sm[:, r, lo:256], ACT.Exp,
                                                        bias=bs[:, w4, 1:2], scale=-1.0,
                                                        accum_out=zf[:, i % 2, 32 + c:33 + c]))

                def turn(t):
                    i, hh, g = jobs[t]
                    s = stt[t]
                    r = t % 3
                    n, p, f = RF.take()
                    for j in range(i + 1):
                        pe = T(lambda e, j=j: e.transpose(p[:, 128 * j:128 * j + 128],
                                                          ef[:, r, 128 * j:128 * j + 128], ident[:]), s["exp"], f)
                    n2, p2, f2 = RT.take()
                    for j in range(0 if i else 1, 2):
                        pe2 = T(lambda e, j=j: e.transpose(p2[:, 128 * j:128 * j + 128],
                                                           es[:, r, 128 * j:128 * j + 128], ident[:]), f2)
                    s["tr"] = pe2
                    pold = stt[t - 3].get("pv") if t >= 3 else T.mark()
                    nk = 128 * (i + 1)
                    lo = 0 if i else 128
                    qf, qt = (A, V) if t % 2 else (V, A)
                    s["e1"] = RF.free[n] = evac(qf, tf[:, r, 0:nk], p[:, 0:nk], pe, pold)
                    s["e2"] = RT.free[n2] = evac(qt, ts_[:, r, lo:256], p2[:, lo:256], pe2, pold)

                obank = {}

                def apply(t):
                    i, hh, g = jobs[t]
                    s = stt[t]
                    r = t % 3
                    if hh == 0 and g == 0:
                        obank[i] = RO.take()
                    n, p, f = obank[i]
                    c = 8 * (4 * hh + g)
                    for j in range(i + 1):
                        T(lambda e, j=j: e.matmul(p[:, c:c + 8], tf[:, r, 128 * j:128 * j + 128],
                                                  vt[:, j, 8 * hh:8 * hh + 8], start=(j == 0), stop=(j == i)),
                          s["e1"], m_vt, f)
                    for j in range(0 if i else 1, 2):
                        s["pv"] = T(lambda e, j=j: e.matmul(p[:, 256 + c:264 + c], ts_[:, r, 128 * j:128 * j + 128],
                                                            vt[:, i - 1 + j, 8 * hh:8 * hh + 8],
                                                            start=(j == (0 if i else 1)), stop=(j == 1)), s["e2"])
                    if hh == 7 and g == 3:
                        finish(i, s["pv"], s["exp"])

                zfree = {}

                def finish(i, pe, ex):
                    n, p, f = obank[i]
                    V(lambda e: e.reciprocal(z4[:, 4:6, :].rearrange("p a b -> p (a b)"), zf[:, i % 2, :]), ex)
                    V(lambda e: e.tensor_tensor(z4[:, 4, :], z4[:, 4, :], gt[:, i, 1:96:3], ALU.mult))
                    V(lambda e: e.tensor_tensor(z4[:, 5, :], z4[:, 5, :], gt[:, i, 2:96:3], ALU.mult))
                    zfree[i % 2] = V.mark()
                    for j in range(2):
                        v = V(lambda e, j=j: e.tensor_tensor(
                            tmp[:].rearrange("p (a d) -> p a d", d=8),
                            p[:, 256 * j:256 * j + 256].rearrange("p (a d) -> p a d", d=8),
                            z4[:, 4 + j, :].unsqueeze(2).to_broadcast([128, 32, 8]), ALU.mult), pe)
                        v = V(lambda e: e.tensor_tensor(acc[:, i, :], acc[:, i, :], tmp[:], ALU.add))
                    RO.free[n] = v
                    n, p, f = RF.take()
                    for k in range(2):
                        pe = T(lambda e, k=k: e.transpose(p[:, 128 * k:128 * k + 128],
                                                          acc[:, i, 128 * k:128 * k + 128], ident[:]), v, f)
                    v = RF.free[n] = V(lambda e: e.tensor_copy(oT[:].rearrange("p a b -> p (a b)"), p[:, 0:256]), pe)
                    n2, p2, f2 = RF.take()
                    for k in range(2):
                        pe = T(lambda e, k=k: e.matmul(p2[:, 0:256], oT[:, k, :], wo[:, k, :], start=(k == 0),
                                                       stop=(k == 1)), v, f2)
                    RF.free[n2] = add_gated(4 * b + i, p2[:, 0:256], pe, tmp[:])

                for t in range(N + 3):
                    if t < N:
                        score(t)
                    if 2 <= t < N + 2:
                        turn(t - 2)
                    if t >= 3:
                        apply(t - 3)
                x_done[b] = SP.dma(xout[:, 4 * b:4 * b + 4, :], Xa[:, 4 * (b % 2):4 * (b % 2) + 4, :], c_o, V.mark())

        def phase_b(ctx):
            def sb(n, shape, dt=F32):
                return sbt(ctx, "b_" + n, shape, dt)

            wmod = sb("wmod", [128, 2, 768])
            iota = sb("iota", [128, 32])
            ti = sb("ti", [128, 16, 4], I32)
            tx = sb("tx", [128, 16, 4])
            tw = sb("tw", [128, 16, 4])
            rw = sb("rw", [128, 16, 32])
            oh = sb("oh", [128, 16, 32])
            SP.dma(wmod[:], D["wmod0b"], c_w)
            SP.dma(iota[:], D["iota"], c_w)
            SP.dma(ti[:], D["tidx"].rearrange("(i p) k -> p i k", p=128), c_w)
            w = SP.dma(tw[:], D["tw"].rearrange("(i p) k -> p i k", p=128), c_w)
            h = sb("h", [128, 4, 256])
            hT = sb("hT", [128, 2, 2048])
            acc = sb("acc", [128, 16, 256])
            gb = sb("gb", [128, 4, 256])
            we = sb("we", [128, 3, 768])
            sg = sb("sg", [128, 3, 512])
            hm = sb("hm", [128, 3, 512])
            tmp = sb("tmp", [128, 256])
            wfree = [None] * 3
            wm = {}

            def load(ex):
                r = ex % 3
                wm[ex] = SP.dma(we[:, r, :], D["exp0"][ex], c_e[r], wfree[r])

            for ex in range(3):
                load(ex)
            V(lambda e: e.memset(acc[:], 0.0))
            V(lambda e: e.tensor_copy(tx[:], ti[:]), w)
            for k in range(4):
                V(lambda e, k=k: e.tensor_tensor(oh[:], iota[:].unsqueeze(1).to_broadcast([128, 16, 32]),
                                                 tx[:, :, k:k + 1].to_broadcast([128, 16, 32]), ALU.is_equal))
                d = rw if k == 0 else oh
                V(lambda e, k=k, d=d: e.tensor_tensor(d[:], oh[:], tw[:, :, k:k + 1].to_broadcast([128, 16, 32]),
                                                      ALU.mult))
                if k:
                    V(lambda e: e.tensor_tensor(rw[:], rw[:], oh[:], ALU.add))
            RG = Ring([PS[:, i, :] for i in range(4)])
            RD = Ring([PS[:, 4 + i, :] for i in range(4)])
            for b in range(4):
                mod_rows(0, b, wmod, w, RG)
                V(lambda e, b=b: e.tensor_copy(gb[:, b, :], mb[:, 2, :]))
                lv = layernorm(b, h, T.mark())
                hr = to_columns(h, hT, 512 * b, RG, lv)
            jobs = [(ex, c) for ex in range(32) for c in range(4)]
            st = [dict() for _ in jobs]

            def up(t):
                ex, c = jobs[t]
                r, r3 = ex % 3, t % 3
                ps = []
                for o in (0, 128):
                    n, p, f = RG.take()
                    for k in range(2):
                        pe = T(lambda e, k=k, o=o, p=p: e.matmul(
                            p[:, :], we[:, r, 256 * k + o:256 * k + o + 128], hT[:, k, 512 * c:512 * c + 512],
                            start=(k == 0), stop=(k == 1)), hr, wm[ex], f)
                    ps.append((n, p, pe))
                (n1, p1, e1), (n2, p2, e2) = ps
                a = RG.free[n1] = A(lambda e: e.activation(sg[:, r3, :], p1[:, :], ACT.Silu), e1,
                                    st[t - 3]["hm"] if t >= 3 else None)
                st[t]["hm"] = RG.free[n2] = V(lambda e: e.tensor_tensor(hm[:, r3, :], sg[:, r3, :], p2[:, :], ALU.mult),
                                              a, e2, st[t - 3]["pe"] if t >= 3 else None)

            def down(t):
                ex, c = jobs[t]
                r, r3 = ex % 3, t % 3
                for i in range(4):
                    n, p, f = RD.take()
                    pe = T(lambda e, i=i, p=p: e.matmul(p[:, 0:256], hm[:, r3, 128 * i:128 * i + 128],
                                                        we[:, r, 512:768], start=True, stop=True), st[t]["hm"], f)
                    g = 4 * c + i
                    RD.free[n] = V(lambda e, p=p, g=g: e.scalar_tensor_tensor(
                        acc[:, g, :], p[:, 0:256], rw[:, g, ex:ex + 1], acc[:, g, :], ALU.mult, ALU.add), pe)
                st[t]["pe"] = pe
                if c == 3:
                    wfree[r] = pe
                    if ex + 3 < 32:
                        load(ex + 3)

            for t in range(len(jobs) + 1):
                if t < len(jobs):
                    up(t)
                if t:
                    down(t - 1)
            for b in range(4):
                for i in range(4):
                    V(lambda e, b=b, i=i: e.tensor_tensor(tmp[:], acc[:, 4 * b + i, :], gb[:, b, :], ALU.mult))
                    V(lambda e, b=b, i=i: e.tensor_tensor(X(4 * b + i), X(4 * b + i), tmp[:], ALU.add))

        def phase_c(ctx):
            def sb(n, shape, dt=F32):
                return sbt(ctx, "c_" + n, shape, dt)

            wmod = sb("wmod", [128, 2, 768])
            wa = sb("wa", [128, 2, 768])
            ba = sb("ba", [128, 4])
            bv = sb("bv", [1, 256])
            wp = sb("wp", [128, 2, 256])
            bp = sb("bp", [1, 256])
            cg = sb("cg", [128, 1])
            lw = sb("lw", [128, 4])
            for t, n in ((wmod, "wmod1a"), (wa, "wa1"), (ba, "ba1"), (bv, "bv1"), (wp, "wp1"), (bp, "bp1"), (cg, "cg1")):
                SP.dma(t[:], D[n], c_w)
            SP.dma(lw[:, 0:1], D["cw0"], c_w)
            w = SP.dma(lw[:, 1:2], D["cw1c"], c_w)
            v = V(lambda e: e.scalar_tensor_tensor(lw[:, 2:3], lw[:, 1:2], 0.5, lw[:, 0:1], ALU.mult, ALU.add), w)
            m_lw = A(lambda e: e.activation(lw[:, 3:4], lw[:, 2:3], ACT.Sigmoid), v)
            h = sb("h", [128, 4, 256])
            hT = sb("hT", [128, 2, 512])
            QK = sb("QK", [128, 4, 512])
            Vt = sb("Vt", [128, 4, 256])
            P = sb("P", [128, 4, 512])
            PT = sb("PT", [128, 4, 512])
            tc = sb("tc", [128, 512])
            z = sb("z", [128, 4, 4])
            o = sb("o", [128, 4, 256])
            oT = sb("oT", [128, 2, 512])
            tmp = sb("tmp", [128, 256])
            R = Ring([PS[:, i, :] for i in range(8)])

            def softmax(i, n, p, pe, ta):
                V(lambda e: e.tensor_reduce(z[:, 0, i:i + 1], p[:, :], AX, ALU.max), pe)
                v = V(lambda e: e.tensor_scalar(z[:, 1, i:i + 1], z[:, 0, i:i + 1], -S1, None, ALU.mult))
                R.free[n] = A(lambda e: e.activation(P[:, i, :], p[:, :], ACT.Exp, bias=z[:, 1, i:i + 1], scale=S1,
                                                     accum_out=z[:, 2, i:i + 1]), v, ta)
                return R.free[n]

            def turn_all(ready):
                ms = []
                old = T.mark()
                for j in range(4):
                    n, p, f = R.take()
                    for i in range(4):
                        pe = T(lambda e, i=i, j=j, p=p: e.transpose(p[:, 128 * i:128 * i + 128],
                                                                    P[:, i, 128 * j:128 * j + 128], ident[:]),
                               ready, f)
                    m = R.free[n] = evac((V, A)[j % 2], PT[:, j, :], p[:, :], pe, old)
                    ms.append(m)
                return ms

            for b in range(8):
                mod_rows(1, b, wmod, w, R)
                lv = layernorm(b, h, T.mark())
                hr = to_columns(h, hT, 0, R, lv, T.mark())
                old = T.mark()
                for m in range(4):
                    n, p, f = R.take()
                    for k in range(2):
                        pe = T(lambda e, k=k, m=m, p=p: e.matmul(p[:, :], wa[:, k, 128 * m:128 * m + 128], hT[:, k, :],
                                                                 start=(k == 0), stop=(k == 1)), hr, w, f)
                    m_qk = R.free[n] = V(lambda e, m=m, p=p: e.tensor_scalar(QK[:, m, :], p[:, :], ba[:, m:m + 1], None,
                                                                             ALU.add), pe)
                for i in range(4):
                    n, p, f = R.take()
                    for k in range(2):
                        T(lambda e, k=k, i=i, p=p: e.matmul(p[:, 0:256], hT[:, k, 128 * i:128 * i + 128],
                                                            wa[:, k, 512:768], start=(k == 0), stop=False), f)
                    pe = T(lambda e, p=p: e.matmul(p[:, 0:256], ones[0:1, :], bv[0:1, :], start=False, stop=True),
                           v_ones)
                    m_v = R.free[n] = V(lambda e, i=i, p=p: e.tensor_copy(Vt[:, i, :], p[:, 0:256]), pe)
                old = T.mark()
                ex = []
                for i in range(4):
                    n, p, f = R.take()
                    pe = T(lambda e, i=i, p=p: e.matmul(p[:, :], QK[:, 0, 128 * i:128 * i + 128], QK[:, 2, :],
                                                        start=True, stop=True), m_qk, f)
                    ex.append(softmax(i, n, p, pe, old))
                for i in range(4):
                    V(lambda e, i=i: e.reciprocal(z[:, 3, i:i + 1], z[:, 2, i:i + 1]), ex[i])
                    v = V(lambda e, i=i: e.tensor_scalar(P[:, i, :], P[:, i, :], z[:, 3, i:i + 1], None, ALU.mult))
                pt = turn_all(v)
                n, p, f = R.take()
                for j in range(4):
                    pe = T(lambda e, j=j, p=p: e.matmul(p[:, :], Vt[:, j, 0:128], PT[:, j, :], start=(j == 0),
                                                        stop=(j == 3)), pt, m_v, f)
                a = R.free[n] = A(lambda e, p=p: e.activation(tc[:], p[:, :], ACT.Tanh, scale=cg[:, 0:1]), pe,
                                  V.mark(), T.mark())
                v = V(lambda e: e.tensor_scalar(tc[:], tc[:], lw[:, 3:4], None, ALU.mult), a, m_lw)
                old = T.mark()
                ex = []
                for i in range(4):
                    n, p, f = R.take()
                    qc = slice(128 * i, 128 * i + 128)
                    T(lambda e, qc=qc, p=p: e.matmul(p[:, :], QK[:, 0, qc], QK[:, 2, :], start=True, stop=False), f)
                    T(lambda e, qc=qc, p=p: e.matmul(p[:, :], QK[:, 1, qc], QK[:, 3, :], start=False, stop=False))
                    pe = T(lambda e, qc=qc, p=p: e.matmul(p[:, :], tc[:, qc], QK[:, 2, :], start=False, stop=True), v)
                    ex.append(softmax(i, n, p, pe, old))
                pt = turn_all(ex)
                for i in range(4):
                    n, p, f = R.take()
                    for j in range(4):
                        pe = T(lambda e, j=j, i=i, p=p: e.matmul(p[:, 0:256], PT[:, j, 128 * i:128 * i + 128],
                                                                 Vt[:, j, :], start=(j == 0), stop=(j == 3)), pt, f)
                    V(lambda e, i=i: e.reciprocal(z[:, 3, i:i + 1], z[:, 2, i:i + 1]))
                    v = R.free[n] = V(lambda e, i=i, p=p: e.tensor_scalar(o[:, i, :], p[:, 0:256], z[:, 3, i:i + 1],
                                                                          None, ALU.mult), pe)
                om = to_columns(o, oT, 0, R, v, T.mark())
                for i in range(4):
                    n, p, f = R.take()
                    for k in range(2):
                        T(lambda e, k=k, i=i, p=p: e.matmul(p[:, 0:256], oT[:, k, 128 * i:128 * i + 128], wp[:, k, :],
                                                            start=(k == 0), stop=False), om, f)
                    pe = T(lambda e, p=p: e.matmul(p[:, 0:256], ones[0:1, :], bp[0:1, :], start=False, stop=True))
                    R.free[n] = add_gated(4 * b + i, p[:, 0:256], pe, tmp[:])

        def phase_d(ctx, HT, RW):
            def sb(n, shape, dt=F32):
                return sbt(ctx, "d_" + n, shape, dt)

            wmod = sb("wmod", [128, 2, 768])
            lnw = sb("lnw", [128, 2, 256])
            rot = sb("rot", [128, 3, 512])
            causal = sb("causal", [128, 512])
            iota = sb("iota", [128, 16])
            wv = sb("wv", [128, 2, 512])
            wo = sb("wo", [128, 16, 256])
            wg = sb("wg", [128, 2, 16])
            for t, n in ((lnw, "lnw"), (rot, "rot1"), (causal, "causal"), (wv, "wv1"), (wo, "wo1"), (wg, "wgr")):
                SP.dma(t[:], D[n], c_w)
            SP.dma(iota[:], D["iota"][:, 0:16], c_w)
            w = SP.dma(wmod[:], D["wmod1b"], c_w)
            wh = sb("wh", [128, 2, 2, 768])
            y = sb("y", [128, 4, 256])
            h = sb("h", [128, 4, 256])
            hT = sb("hT", [128, 2, 512])
            qs = sb("qs", [128, 2, 4, 512])
            ks = sb("ks", [128, 2, 512])
            t1 = sb("t1", [128, 2, 512])
            vt = sb("vt", [128, 4, 512])
            fm = sb("fm", [128, 3, 512])
            ef = sb("ef", [128, 3, 512])
            tf = sb("tf", [128, 3, 512])
            bs = sb("bs", [128, 4])
            zz = sb("zz", [128, 4, 4])
            zr = sb("zr", [128, 4])
            o = sb("o", [128, 2, 256])
            oT = sb("oT", [128, 2, 256])
            tmp = sb("tmp", [128, 256])
            rt = sb("rt", [128, 6, 16])
            ri = sb("ri", [128, 8], U32)
            RS = Ring([PS[:, i, :] for i in range(2)])
            RF = Ring([PS[:, 2 + i, :] for i in range(2)])
            RO = Ring([PS[:, 4 + i, 0:256] for i in range(2)])
            Y = [PS[:, 6, 0:256], PS[:, 6, 256:512], PS[:, 7, 0:256], PS[:, 7, 256:512]]
            y_free = None
            n_w = 0
            whfree = [None, None]
            whm = {}

            def load(k):
                whm[k] = SP.dma(wh[:, k % 2, :, :], D["wh1"][k % 8], c_e[k % 2], whfree[k % 2])

            load(0)
            load(1)
            qk_free = [None, None]
            z_free = [None] * 4
            o_free = [None, None]
            oT_free = [None, None]
            hist = []

            def past(t, key):
                return hist[t][key] if t >= 0 else None

            for b in range(8):
                mod_rows(1, b, wmod, w, RS)
                layernorm(b, y)
                lv = rmsnorm(y, lnw[:, 0, :], h, tmp[:], T.mark())
                hr = to_columns(h, hT, 0, RS, lv, T.mark())
                for i in range(4):
                    n, p, f = RS.take()
                    for k in range(2):
                        pe = T(lambda e, k=k, i=i, p=p: e.matmul(p[:, :], hT[:, k, 128 * i:128 * i + 128], wv[:, k, :],
                                                                 start=(k == 0), stop=(k == 1)), hr, w, f)
                    m_v = RS.free[n] = V(lambda e, i=i, p=p: e.tensor_copy(vt[:, i, :], p[:, :]), pe)
                m_q = {}

                def project(hh):
                    kk = 8 * b + hh
                    r = kk % 2
                    for g in range(6):
                        n, p, f = RS.take()
                        for k in range(2):
                            pe = T(lambda e, k=k, g=g, p=p, r=r: e.matmul(
                                p[:, :], wh[:, r, k, 128 * g:128 * g + 128], hT[:, k, :], start=(k == 0),
                                stop=(k == 1)), hr, whm[kk], f)
                        if g < 4:
                            v = V(lambda e, g=g, p=p, r=r: e.tensor_tensor(qs[:, r, g, :], p[:, :], rot[:, 0, :],
                                                                           ALU.mult), pe, qk_free[r])
                        else:
                            v = V(lambda e, g=g, p=p: e.tensor_tensor(t1[:, g - 4, :], p[:, :], rot[:, g - 3, :],
                                                                      ALU.mult), pe)
                        RS.free[n] = v
                    whfree[r] = pe
                    if kk + 2 < 64:
                        load(kk + 2)
                    m_q[hh] = V(lambda e, r=r: e.tensor_tensor(ks[:, r, :], t1[:, 0, :], t1[:, 1, :], ALU.add))

                jobs = [(hh, i, g) for hh in range(8) for i in range(4) for g in range(4)]
                N = len(jobs)
                base = len(hist)
                hist.extend(dict() for _ in jobs)
                grp = {}

                def score(t):
                    hh, i, g = jobs[t]
                    if i == 0 and g == 0:
                        project(hh)
                    s, u = hist[base + t], base + t
                    r = u % 3
                    kr = (8 * b + hh) % 2
                    nk = 128 * (i + 1)
                    n, p, f = RS.take()
                    s["pe"] = T(lambda e: e.matmul(p[:, 0:nk], qs[:, kr, g, 128 * i:128 * i + 128], ks[:, kr, 0:nk],
                                                   start=True, stop=True), m_q[hh], f)
                    if i == 3 and g == 3:
                        qk_free[kr] = s["pe"]
                    s["v"] = RS.free[n] = V(lambda e: e.tensor_tensor_reduce(
                        fm[:, r, 0:nk], p[:, 0:nk], causal[:, 512 - nk:512], -S2, BIG, ALU.add, ALU.min,
                        bs[:, u % 4:u % 4 + 1]), s["pe"], past(u - 3, "exp"))
                    s["exp"] = A(lambda e: e.activation(ef[:, r, 0:nk], fm[:, r, 0:nk], ACT.Exp,
                                                        bias=bs[:, u % 4:u % 4 + 1], scale=-1.0,
                                                        accum_out=zz[:, (u // 4) % 4, g:g + 1]),
                                 s["v"], past(u - 3, "tr"), z_free[(u // 4) % 4])

                def turn(t):
                    hh, i, g = jobs[t]
                    s, u = hist[base + t], base + t
                    r = u % 3
                    nk = 128 * (i + 1)
                    n, p, f = RF.take()
                    for j in range(i + 1):
                        s["tr"] = T(lambda e, j=j: e.transpose(p[:, 128 * j:128 * j + 128],
                                                               ef[:, r, 128 * j:128 * j + 128], ident[:]), s["exp"], f)
                    s["ev"] = RF.free[n] = evac((A, A, V)[u % 3], tf[:, r, 0:nk], p[:, 0:nk], s["tr"],
                                                past(u - 3, "pv"))

                def apply(t):
                    hh, i, g = jobs[t]
                    s, u = hist[base + t], base + t
                    r = u % 3
                    if g == 0:
                        grp[t // 4] = RO.take()
                    n, p, f = grp[t // 4]
                    for j in range(i + 1):
                        s["pv"] = T(lambda e, j=j: e.matmul(p[:, 64 * g:64 * g + 64], tf[:, r, 128 * j:128 * j + 128],
                                                            vt[:, j, 64 * hh:64 * hh + 64], start=(j == 0),
                                                            stop=(j == i)), s["ev"], m_v, f)
                    if g == 3:
                        zi = (u // 4) % 4
                        ro = (u // 4) % 2
                        V(lambda e: e.reciprocal(zr[:], zz[:, zi, :]), s["exp"])
                        v = V(lambda e: e.tensor_tensor(
                            o[:, ro, :].rearrange("p (g d) -> p g d", g=4),
                            p[:, :].rearrange("p (g d) -> p g d", g=4),
                            zr[:].unsqueeze(2).to_broadcast([128, 4, 64]), ALU.mult), s["pv"], o_free[ro])
                        z_free[zi] = RO.free[n] = v
                        s["o"] = v

                def out_turn(t):
                    hh, i, g = jobs[t]
                    s, u = hist[base + t], base + t
                    ro = (u // 4) % 2
                    n, p, f = RF.take()
                    for k in range(2):
                        pe = T(lambda e, k=k: e.transpose(p[:, 128 * k:128 * k + 128],
                                                          o[:, ro, 128 * k:128 * k + 128], ident[:]), s["o"], f)
                    o_free[ro] = pe
                    s["oT"] = RF.free[n] = A(lambda e: e.activation(oT[:, ro, :], p[:, 0:256], ACT.Copy), pe,
                                             oT_free[ro])

                def out_proj(t):
                    hh, i, g = jobs[t]
                    s, u = hist[base + t], base + t
                    ro = (u // 4) % 2
                    for k in range(2):
                        first = hh == 0 and k == 0 and i % 2 == 0
                        pe = T(lambda e, k=k, first=first: e.matmul(
                            Y[i], oT[:, ro, 128 * k:128 * k + 128], wo[:, 2 * hh + k, :],
                            start=first, stop=(hh == 7 and k == 1), skip_group_check=True), s["oT"], y_free)
                    oT_free[ro] = pe
                    return pe

                for t in range(N + 8):
                    if t < N:
                        score(t)
                    if 2 <= t < N + 2:
                        turn(t - 2)
                    if 3 <= t < N + 3:
                        apply(t - 3)
                    if 4 <= t < N + 4 and (t - 4) % 4 == 3:
                        out_turn(t - 4)
                    if 6 <= t < N + 6 and (t - 6) % 4 == 3:
                        pe = out_proj(t - 6)
                for i in range(4):
                    v = V(lambda e, i=i: e.tensor_tensor(y[:, i, :], y[:, i, :], Y[i], ALU.add), pe)
                y_free = v
                lv = rmsnorm(y, lnw[:, 1, :], h, tmp[:], T.mark())
                to_columns(h, HT, 512 * b, RS, lv)
                hw = RS.free[:]
                for i in range(4):
                    V(lambda e, i=i: e.tensor_tensor(tmp[:], y[:, i, :], mb[:, 2, :], ALU.mult))
                    V(lambda e, i=i, b=b: e.tensor_tensor(X(4 * b + i), X(4 * b + i), tmp[:], ALU.add))
                    n, p, f = RS.take()
                    for k in range(2):
                        pe = T(lambda e, k=k, i=i, b=b, p=p: e.matmul(
                            p[:, 0:16], HT[:, k, 512 * b + 128 * i:512 * b + 128 * i + 128], wg[:, k, :],
                            start=(k == 0), stop=(k == 1)), hw, w, f)
                    RS.free[n] = V(lambda e, p=p: e.tensor_copy(rt[:, 0, :], p[:, 0:16]), pe)
                    V(lambda e: e.max(rt[:, 1, 0:8], rt[:, 0, :]))
                    V(lambda e: e.max_index(ri[:], rt[:, 1, 0:8], rt[:, 0, :]))
                    V(lambda e: e.tensor_copy(rt[:, 2, 0:8], ri[:]))
                    v = V(lambda e: e.tensor_scalar(rt[:, 1, 8:9], rt[:, 1, 0:1], -1.0, None, ALU.mult))
                    a = A(lambda e: e.activation(rt[:, 3, 0:4], rt[:, 1, 0:4], ACT.Exp, bias=rt[:, 1, 8:9],
                                                 accum_out=rt[:, 3, 4:5]), v)
                    V(lambda e: e.reciprocal(rt[:, 3, 5:6], rt[:, 3, 4:5]), a)
                    V(lambda e: e.tensor_scalar(rt[:, 3, 8:12], rt[:, 3, 0:4], rt[:, 3, 5:6], None, ALU.mult))
                    for k in range(4):
                        d = RW[:, 4 * b + i, :] if k == 0 else rt[:, 4, :]
                        V(lambda e, k=k, d=d: e.tensor_scalar(d, iota[:], rt[:, 2, k:k + 1], rt[:, 3, 8 + k:9 + k],
                                                              ALU.is_equal, ALU.mult))
                        if k:
                            V(lambda e, b=b, i=i: e.tensor_tensor(RW[:, 4 * b + i, :], RW[:, 4 * b + i, :],
                                                                  rt[:, 4, :], ALU.add))

        def phase_e(ctx, HT, RW):
            def sb(n, shape, dt=F32):
                return sbt(ctx, "e_" + n, shape, dt)

            wmod = sb("wmod", [128, 2, 768])
            w = SP.dma(wmod[:], D["wmod1b"], c_w)
            acc = sb("acc", [128, 32, 256])
            we = sb("we", [128, 3, 1536])
            sg = sb("sg", [128, 4, 512])
            hm = sb("hm", [128, 4, 2, 512])
            tmp = sb("tmp", [128, 256])
            wfree = [None] * 3
            wm = {}

            def load(ex):
                r = ex % 3
                wm[ex] = SP.dma(we[:, r, :], D["exp1"][ex], c_e[r], wfree[r])

            for ex in range(3):
                load(ex)
            V(lambda e: e.memset(acc[:], 0.0))
            RG = Ring([PS[:, i, :] for i in range(4)])
            RD = Ring([PS[:, 4 + i, :] for i in range(4)])
            jobs = [(ex, c) for ex in range(16) for c in range(8)]
            st = [dict() for _ in jobs]
            hist = []

            def up(t):
                ex, c = jobs[t]
                r, r4 = ex % 3, t % 4
                for m in range(2):
                    ps = []
                    for o in (0, 256):
                        n, p, f = RG.take()
                        for k in range(2):
                            c0 = 512 * k + o + 128 * m
                            pe = T(lambda e, k=k, c0=c0, p=p: e.matmul(
                                p[:, :], we[:, r, c0:c0 + 128], HT[:, k, 512 * c:512 * c + 512],
                                start=(k == 0), stop=(k == 1)), wm[ex], f)
                        ps.append((n, p, pe))
                    (n1, p1, e1), (n2, p2, e2) = ps
                    u = len(hist)
                    a = RG.free[n1] = A(lambda e, u=u, p1=p1: e.activation(sg[:, u % 4, :], p1[:, :], ACT.Silu), e1,
                                        hist[u - 4] if u >= 4 else None)
                    v = RG.free[n2] = V(lambda e, u=u, m=m, p2=p2: e.tensor_tensor(
                        hm[:, r4, m, :], sg[:, u % 4, :], p2[:, :], ALU.mult), a, e2,
                        st[t - 4]["pe"] if t >= 4 else None)
                    hist.append(v)
                st[t]["hm"] = v

            def down(t):
                ex, c = jobs[t]
                r, r4 = ex % 3, t % 4
                for i in range(4):
                    n, p, f = RD.take()
                    for k in range(2):
                        pe = T(lambda e, i=i, k=k, p=p: e.matmul(
                            p[:, 0:256], hm[:, r4, k, 128 * i:128 * i + 128],
                            we[:, r, 1024 + 256 * k:1280 + 256 * k], start=(k == 0), stop=(k == 1)), st[t]["hm"], f)
                    g = 4 * c + i
                    RD.free[n] = V(lambda e, p=p, g=g: e.scalar_tensor_tensor(
                        acc[:, g, :], p[:, 0:256], RW[:, g, ex:ex + 1], acc[:, g, :], ALU.mult, ALU.add), pe)
                st[t]["pe"] = pe
                if c == 7:
                    wfree[r] = pe
                    if ex + 3 < 16:
                        load(ex + 3)

            for t in range(len(jobs) + 1):
                if t < len(jobs):
                    up(t)
                if t:
                    down(t - 1)
            for b in range(8):
                mod_rows(1, b, wmod, w, RG)
                for i in range(4):
                    g = 4 * b + i
                    V(lambda e, g=g: e.tensor_tensor(tmp[:], acc[:, g, :], mb[:, 2, :], ALU.mult))
                    v = V(lambda e, g=g: e.tensor_tensor(X(g), X(g), tmp[:], ALU.add))
                SP.dma(xout[:, 4 * b:4 * b + 4, :], home["at"][:, 4 * b:4 * b + 4, :], c_o, v)

        with ExitStack() as ctx:
            phase_a(ctx)
        fence()
        Xs = sbt(top, "X", [128, 32, 256])
        m_x = SP.dma(Xs[:], xout, c_x)
        home.update(at=Xs, n=32, ready=lambda b: m_x)
        for phase in (phase_b, phase_c):
            with ExitStack() as ctx:
                phase(ctx)
            fence()
        with ExitStack() as keep:
            HT = sbt(keep, "HT", [128, 2, 4096])
            RW = sbt(keep, "RW", [128, 32, 16])
            with ExitStack() as ctx:
                phase_d(ctx, HT, RW)
            fence()
            with ExitStack() as ctx:
                phase_e(ctx, HT, RW)
            fence()


def layouts(I):
    d = {}

    def two(w):
        return np.ascontiguousarray(w.reshape(2, 128, -1).transpose(1, 0, 2))

    d["x"] = I["L0_attn_hidden_states"]
    d["c0"] = np.ascontiguousarray(I["L0_c"].T.reshape(2, 128, 8).transpose(1, 0, 2))
    d["c1"] = np.ascontiguousarray(I["L1_c"].T.reshape(2, 128, 8).transpose(1, 0, 2))
    for n in "01":
        d[f"wmod{n}a"], d[f"wmod{n}b"] = two(I[f"L{n}_wmod"][:, 0:768]), two(I[f"L{n}_wmod"][:, 768:1536])
    wqkv = I["L0_attn_w_qkv"]
    wq = np.zeros((256, 8, 4, 32), np.float32)
    wkA = np.zeros((256, 8, 4, 32), np.float32)
    wkB = np.zeros((256, 8, 4, 32), np.float32)
    q = wqkv[:, 0:256].reshape(256, 8, 4, 8)
    k = wqkv[:, 256:320].reshape(256, 8, 1, 8)
    sw = np.array([1, 0, 3, 2, 5, 4, 7, 6])
    wq[..., 0:8] = q
    wq[..., 8:16] = q[..., sw]
    wq[..., 16:24] = q
    for o in (0, 8):
        wkA[..., o:o + 8] = k
        wkB[..., o:o + 8] = k[..., sw]
    d["wq0"], d["wkA0"], d["wkB0"] = two(wq), two(wkA), two(wkB)
    d["wkv0"] = two(wqkv[:, 256:384])
    d["wg0"] = two(I["L0_attn_w_gate"])
    d["bg0"] = I["L0_attn_b_gate"].reshape(1, 96)
    d["wo0"] = two(I["L0_attn_w_out"])
    d["cw1"] = np.stack([I[f"L0_attn_{n}_cw1"].reshape(16, 8, 128).transpose(1, 0, 2) for n in "kv"], 1)
    d["kvpos"] = np.stack([I[f"L0_attn_{n}_pos"].transpose(2, 1, 0) for n in "kv"], 1)
    d["cb1"] = np.stack([I[f"L0_attn_{n}_cb1"] for n in "kv"], 1)
    w2 = np.zeros((128, 4, 32), np.float32)
    w2[:, :, 16:24] = I["L0_attn_k_cw2"][:, None, :]
    d["cw2k"] = w2.reshape(128, 128)
    b2 = np.zeros((4, 32), np.float32)
    b2[:, 16:24] = I["L0_attn_k_cb2"][None]
    d["cb2k"] = b2.reshape(128, 1)
    d["cw2v"] = I["L0_attn_v_cw2"]
    d["cb2v"] = np.tile(I["L0_attn_v_cb2"][None], (128, 1))
    mc = np.zeros((4, 32, 8), np.float32)
    mc[:, 16:24, :] = I["L0_attn_mem_ck"][:, 0, :].T[None]
    d["mck"] = mc.reshape(128, 8)
    d["mcv"] = np.tile(I["L0_attn_mem_cv"].reshape(1, 8, 8), (128, 1, 1))
    d["tidx"] = I["L0_ffn_topk_idx"]
    d["tw"] = I["L0_ffn_topk_weight"]
    e = np.zeros((32, 128, 768), np.float32)
    g = I["L0_ffn_gate_weight"].transpose(0, 2, 1).reshape(32, 2, 128, 128)
    u = I["L0_ffn_up_weight"].transpose(0, 2, 1).reshape(32, 2, 128, 128)
    for kk in range(2):
        e[:, :, 256 * kk:256 * kk + 128] = g[:, kk]
        e[:, :, 256 * kk + 128:256 * kk + 256] = u[:, kk]
    e[:, :, 512:768] = I["L0_ffn_down_weight"].transpose(0, 2, 1)
    d["exp0"] = e
    d["wa1"] = two(I["L1_attn_c_attn_w"])
    ba = I["L1_attn_c_attn_b"]
    d["ba1"] = ba[0:512].reshape(4, 128).T
    d["bv1"] = ba[512:768].reshape(1, 256)
    d["wp1"] = two(I["L1_attn_c_proj_w"])
    d["bp1"] = I["L1_attn_c_proj_b"].reshape(1, 256)
    d["cg1"] = I["L1_attn_cam_gate"].reshape(128, 1)
    d["cw0"] = np.tile(I["L1_attn_cam_w0"].reshape(1, 1), (128, 1))
    d["cw1c"] = np.tile(I["L1_attn_cam_w1"].reshape(1, 1), (128, 1))
    d["lnw"] = np.tile(np.stack([I["L1_ffn_ln_w"], I["L1_ffn_ff_ln_w"]])[None], (128, 1, 1))
    wq = I["L1_ffn_wq"].reshape(256, 8, 4, 2, 32)
    wk = I["L1_ffn_wk"].reshape(256, 8, 2, 32)
    wh = np.zeros((256, 8, 6, 4, 32), np.float32)
    for s in range(2):
        wh[:, :, 0:4, s] = wq[:, :, :, s]
        wh[:, :, 0:4, 2 + s] = wq[:, :, :, 1 - s]
        for o in (0, 2):
            wh[:, :, 4, o + s] = wk[:, :, s]
            wh[:, :, 5, o + s] = wk[:, :, 1 - s]
    d["wh1"] = wh.reshape(2, 128, 8, 768).transpose(2, 1, 0, 3)
    d["wv1"] = two(I["L1_ffn_wv"])
    d["wo1"] = I["L1_ffn_wo"].reshape(16, 128, 256).transpose(1, 0, 2)
    d["wgr"] = two(I["L1_ffn_wg"])
    e = np.zeros((16, 128, 1536), np.float32)
    w1 = I["L1_ffn_w1"].reshape(16, 2, 128, 256)
    w3 = I["L1_ffn_w3"].reshape(16, 2, 128, 256)
    w2 = I["L1_ffn_w2"].reshape(16, 2, 128, 256)
    for kk in range(2):
        e[:, :, 512 * kk:512 * kk + 256] = w1[:, kk]
        e[:, :, 512 * kk + 256:512 * kk + 512] = w3[:, kk]
        e[:, :, 1024 + 256 * kk:1280 + 256 * kk] = w2[:, kk]
    d["exp1"] = e
    d.update(consts())
    return {k: np.ascontiguousarray(v) for k, v in d.items()}


def kernel(**inputs):
    import concourse.bacc as _bacc
    from concourse.bass_utils import run_bass_kernel_spmd as _run

    nc = _bacc.Bacc("TRN2", target_bir_lowering=False, num_devices=1)
    arrays, aps = {}, {}
    for name, a in layouts({k: np.asarray(v) for k, v in inputs.items()}).items():
        arrays["in_" + name] = a
        aps[name] = nc.dram_tensor("in_" + name, a.shape, mybir.dt.from_np(a.dtype), kind="ExternalInput").ap()
    out = nc.dram_tensor("out_0", (8, 512, 256), F32, kind="ExternalOutput").ap()
    program(nc, aps, out)
    r = _run(nc, [arrays], core_ids=[0])
    return r.results[0]["out_0"]
```

```python
import math
from contextlib import ExitStack

import numpy as np
import concourse.bass as bass
from concourse import mybir

F32 = mybir.dt.float32
BF16 = mybir.dt.bfloat16
U32 = mybir.dt.uint32
I32 = mybir.dt.int32
ALU = mybir.AluOpType
ACT = mybir.ActivationFunctionType
AX = mybir.AxisListType.X
NEG = -1e30
BIG = 3.0e38
EPS = 1e-5
S0 = 8 ** -0.5
S1 = 0.25
S2 = 0.125


def flat(ws):
    for w in ws:
        if w is None:
            continue
        if isinstance(w, list):
            yield from flat(w)
        else:
            yield w


class Queue:

    def __init__(self, eng, sem, chained=False):
        self.eng, self.sem, self.n, self.seen, self.chained = eng, sem, 0, {}, chained

    def wait(self, *marks):
        for sem, v in flat(marks):
            if self.seen.get(sem, 0) < v:
                self.seen[sem] = v
                self.eng.wait_ge(sem, v)

    def __call__(self, fn, *marks):
        if self.chained:
            self.wait(self.mark())
        self.wait(*marks)
        self.n += 1
        fn(self.eng).then_inc(self.sem, 1)
        return self.mark()

    def mark(self):
        return (self.sem, self.n)

    def dma(self, out, in_, count, *marks):
        self.wait(*marks)
        count.n += 16
        self.eng.dma_start(out, in_).then_inc(count.sem, 16)
        return (count.sem, count.n)


class Count:
    def __init__(self, sem):
        self.sem, self.n = sem, 0

    def mark(self):
        return (self.sem, self.n)


class Ring:

    def __init__(self, bufs):
        self.bufs, self.free, self.k = bufs, [None] * len(bufs), 0

    def take(self):
        i = self.k % len(self.bufs)
        self.k += 1
        return i, self.bufs[i], self.free[i]


def consts():
    c = {}
    c["ident"] = np.eye(128, dtype=np.float32)
    pos = np.arange(512, dtype=np.float32)
    inv = (1.0 / 10000.0 ** (np.arange(0, 8, 2, dtype=np.float32) / 8)).astype(np.float32)
    ang = (pos[:, None] * inv[None, :]).astype(np.float32)
    cos, sin = np.cos(ang).astype(np.float32), np.sin(ang).astype(np.float32)
    rot = np.zeros((128, 2, 512), np.float32)
    for r in range(128):
        d = r % 8
        rot[r, 0] = cos[:, d // 2]
        rot[r, 1] = (-1.0 if d % 2 == 0 else 1.0) * sin[:, d // 2]
    c["rot0"] = rot
    inv = (1.0 / 150000.0 ** (np.arange(32, dtype=np.float32) / 32)).astype(np.float32)
    ang = (pos[:, None] * inv[None, :]).astype(np.float32)
    cos, sin = np.cos(ang).astype(np.float32), np.sin(ang).astype(np.float32)
    csq = np.zeros((128, 512), np.float32)
    cok = np.zeros((128, 512), np.float32)
    sik = np.zeros((128, 512), np.float32)
    for d in range(64):
        sg = -1.0 if d < 32 else 1.0
        csq[d] = cos[:, d % 32]
        csq[64 + d] = sg * sin[:, d % 32]
        for o in (0, 64):
            cok[o + d] = cos[:, d % 32]
            sik[o + d] = sg * sin[:, d % 32]
    c["rot1"] = np.stack([csq, cok, sik], 1)
    p = np.arange(128)
    bf = np.dtype("bfloat16")
    k = np.arange(128)
    cm = np.where((k[None] // 16 == p[:, None] // 16) & (k[None] > p[:, None]), NEG, 0.0)
    c["cmask"] = cm.astype(bf)
    c["cmaskT"] = np.tile(cm.T, (1, 4)).astype(bf)
    k = np.arange(256)
    dl = 128 + p[:, None] - k[None]
    sm = np.where((dl >= 0) & (dl <= 64), 0.0, NEG)
    c["smask"] = np.stack([sm[:, 64:]] * 2, 1).astype(bf)
    c["smaskT"] = np.stack([np.tile(sm[:, 128 * j:128 * j + 128].T, (1, 4)) for j in range(2)], 1).astype(bf)
    c["identb"] = np.eye(128).astype(bf)
    kr = np.zeros((2, 51, 8, 512), np.float32)
    for t in range(512):
        kr[0, t // 16, :, t] = 1.0
    kr[0, 32:35] = 1.0
    kr[1, 48:51] = 1.0
    c["keyrows"] = kr.astype(bf)
    c["diag16"] = (p[:, None] // 8 == np.arange(16)[None]).astype(np.float32)
    no = np.ones((128, 4, 32), np.float32)
    for i in range(4):
        no[p, i, 8 * i + p // 16] = 0.0
    c["notown"] = no
    causal = np.zeros((128, 512), np.float32)
    causal[:, 384:] = np.where(np.arange(128)[None] <= p[:, None], 0.0, NEG)
    c["causal"] = causal
    mc = np.zeros((128, 4, 33), np.float32)
    last = np.concatenate([[-1], (np.arange(32) + 1) * 16 - 1])
    for i in range(4):
        mc[:, i] = np.where(last[None] < (128 * i + p)[:, None], 0.0, NEG)
    c["maskc"] = mc
    c["iota"] = np.tile(np.arange(32, dtype=np.float32), (128, 1))
    return c


def program(nc, D, out):
    with ExitStack() as top:
        def sem(n):
            return top.enter_context(nc.semaphore(n))

        def sbt(ctx, n, shape, dt=F32):
            return ctx.enter_context(nc.sbuf_tensor(n, shape, dt))

        V = Queue(nc.vector, sem("s_vec"), True)
        G = Queue(nc.gpsimd, sem("s_pool"), True)
        A = Queue(nc.scalar, sem("s_act"))
        T = Queue(nc.tensor, sem("s_pe"))
        SP = Queue(nc.sync, sem("s_sp"))
        c_w = Count(sem("c_w"))
        c_c = Count(sem("c_c"))
        c_x = Count(sem("c_x"))
        c_xa = [Count(sem(f"c_xa{i}")) for i in range(2)]
        c_k = Count(sem("c_k"))
        c_q = [Count(sem(f"c_q{i}")) for i in range(2)]
        c_k6 = [Count(sem(f"c_k6{i}")) for i in range(2)]
        c_s = Count(sem("c_s"))
        c_m = [Count(sem(f"c_m{i}")) for i in range(2)]
        c_h = [Count(sem(f"c_h{i}")) for i in range(2)]
        c_e = [Count(sem(f"c_e{i}")) for i in range(3)]
        c_o = Count(sem("c_o"))

        def fence():
            marks = [q.mark() for q in (V, G, A, T)] + [c.mark() for c in (c_c, c_w, c_x, c_k, c_o, c_s, *c_q, *c_k6, *c_e, *c_xa, *c_m, *c_h)]
            for q in (V, G, A, T, SP):
                q.wait(marks)

        PS = top.enter_context(nc.psum_tensor("PS", [128, 8, 512], F32))
        ident = sbt(top, "ident", [128, 128])
        ones = sbt(top, "ones", [128, 128])
        silu = sbt(top, "silu", [128, 2, 2, 8])
        mb2 = sbt(top, "mb", [128, 2, 3, 256])
        mb = mb2[:, 0, :, :]
        mtmp = sbt(top, "mtmp", [128, 2, 256])
        cbt = sbt(top, "cbt", [128, 2, 128])
        st6 = sbt(top, "st6", [128, 4, 6])
        mv = sbt(top, "mv", [128, 4, 2])
        rs = sbt(top, "rs", [128, 3, 4])

        xin = D["x"].rearrange("b (i p) d -> p (b i) d", p=128)
        xout = out.rearrange("b (i p) d -> p (b i) d", p=128)
        SP.dma(ident[:], D["ident"], c_c)
        SP.dma(silu[:, 0, :, :], D["c0"], c_c)
        w_c = SP.dma(silu[:, 1, :, :], D["c1"], c_c)
        home = {}

        def X(g):
            return home["at"][:, g % home["n"], :]

        v_ones = V(lambda e: e.memset(ones[:], 1.0))
        sl = silu[:].rearrange("p a b c -> p (a b c)")
        a_silu = A(lambda e: e.activation(sl, sl, ACT.Silu), w_c)

        def mod_rows(layer, b, wmod, wready, ring, mb=mb):
            for k in range(2):
                vb = V(lambda e, k=k: e.tensor_scalar(cbt[:, k, :], ones[:], silu[:, layer, k, b:b + 1], None,
                                                      ALU.mult), a_silu, T.mark())
            i1, p1, f1 = ring.take()
            i2, p2, f2 = ring.take()
            for o, n, p in ((0, 512, p1), (512, 256, p2)):
                for k in range(2):
                    pe = T(lambda e, k=k, o=o, n=n, p=p: e.matmul(
                        p[:, 0:n], cbt[:, k, :], wmod[:, k, o:o + n],
                        start=(k == 0), stop=(k == 1)), vb, wready, f1, f2)
            V(lambda e: e.tensor_copy(mb[:, 0, :], p1[:, 0:256]), pe)
            ring.free[i1] = V(lambda e: e.tensor_scalar(mb[:, 1, :], p1[:, 256:512], 1.0, None, ALU.add))
            V(lambda e: e.tensor_scalar(mtmp[:, 0, :], p2[:, 0:256], 0.0, 2.0, ALU.is_ge, ALU.mult))
            ring.free[i2] = V(lambda e: e.tensor_scalar(mtmp[:, 1, :], p2[:, 0:256], -1.0, None, ALU.mult))
            V(lambda e: e.tensor_tensor(mtmp[:, 1, :], p2[:, 0:256], mtmp[:, 1, :], ALU.max))
            V(lambda e: e.tensor_scalar(mtmp[:, 1, :], mtmp[:, 1, :], 0.25, None, ALU.max))
            v = V(lambda e: e.scalar_tensor_tensor(mb[:, 2, :], mtmp[:, 0, :], -1.0, mtmp[:, 1, :],
                                                   ALU.add, ALU.mult))
            ring.free[i1] = ring.free[i2] = v
            return v

        def layernorm(b, dst, *marks, mb=mb):
            for i in range(4):
                V(lambda e, i=i: e.bn_stats(st6[:, i, :], X(4 * b + i)), home["ready"](b))
                V(lambda e, i=i: e.bn_aggr(mv[:, i, :], st6[:, i, :]))
            v = V(lambda e: e.tensor_scalar(rs[:, 0, :], mv[:, :, 1], EPS, None, ALU.add))
            a = A(lambda e: e.activation(rs[:, 1, :], rs[:, 0, :], ACT.Sqrt), v)
            V(lambda e: e.reciprocal(rs[:, 2, :], rs[:, 1, :]), a)
            for i in range(4):
                V(lambda e, i=i: e.tensor_scalar(dst[:, i, :], X(4 * b + i), mv[:, i, 0:1],
                                                 rs[:, 2, i:i + 1], ALU.subtract, ALU.mult), *marks)
                V(lambda e, i=i: e.tensor_tensor(dst[:, i, :], dst[:, i, :], mb[:, 1, :], ALU.mult))
                v = V(lambda e, i=i: e.tensor_tensor(dst[:, i, :], dst[:, i, :], mb[:, 0, :], ALU.add))
            return v

        def rmsnorm(src, w, dst, sq, *marks):
            for i in range(4):
                V(lambda e, i=i: e.tensor_tensor(sq, src[:, i, :], src[:, i, :], ALU.mult), *marks)
                V(lambda e, i=i: e.tensor_reduce(rs[:, 1, i:i + 1], sq, AX, ALU.add))
            v = V(lambda e: e.tensor_scalar(rs[:, 0, :], rs[:, 1, :], 1.0 / 256, EPS, ALU.mult, ALU.add))
            a = A(lambda e: e.activation(rs[:, 1, :], rs[:, 0, :], ACT.Sqrt), v)
            V(lambda e: e.reciprocal(rs[:, 2, :], rs[:, 1, :]), a)
            for i in range(4):
                v = V(lambda e, i=i: e.scalar_tensor_tensor(dst[:, i, :], src[:, i, :], rs[:, 2, i:i + 1], w,
                                                            ALU.mult, ALU.mult))
            return v

        def to_columns(src, dst, at, ring, ready, *marks):
            for k in range(2):
                n, p, f = ring.take()
                for i in range(4):
                    pe = T(lambda e, i=i, k=k, p=p: e.transpose(
                        p[:, 128 * i:128 * i + 128], src[:, i, 128 * k:128 * k + 128], ident[:]),
                        ready, f, w_c)
                q = (V, A)[k]
                if k == 0:
                    m0 = V(lambda e, k=k, p=p: e.tensor_copy(dst[:, k, at:at + 512], p[:, :]), pe, *marks)
                    ring.free[n] = m0
                else:
                    m1 = A(lambda e, k=k, p=p: e.activation(dst[:, k, at:at + 512], p[:, :], ACT.Copy), pe, *marks)
                    ring.free[n] = m1
            return [m0, m1]

        def add_gated(tile, psum, pe, tmp, mb=mb):
            V(lambda e: e.tensor_tensor(tmp, psum, mb[:, 2, :], ALU.mult), pe)
            return V(lambda e: e.tensor_tensor(X(tile), X(tile), tmp, ALU.add))

        def evac(q, out_, in_, *marks):
            if q is V:
                return V(lambda e: e.tensor_copy(out_, in_), *marks)
            return A(lambda e: e.activation(out_, in_, ACT.Copy), *marks)

        def phase_a(ctx):
            def sb(n, shape, dt=F32):
                return sbt(ctx, "a_" + n, shape, dt)

            wmod = sb("wmod", [128, 2, 768])
            wq = sb("wq", [128, 2, 704])
            wg = sb("wg", [128, 2, 96])
            bg = sb("bg", [1, 96])
            wo = sb("wo", [128, 2, 256])
            cw1 = sb("cw1", [40, 16, 128])
            pos = sb("pos", [40, 16, 8])
            cb1 = sb("cb1", [128, 2])
            cw2k = sb("cw2k", [128, 128])
            cb2k = sb("cb2k", [128, 1])
            cw2v = sb("cw2v", [128, 8])
            cb2v = sb("cb2v", [128, 8])
            mck = sb("mck", [128, 8])
            mcv = sb("mcv", [128, 8, 8])
            rot = sb("rot", [128, 2, 512])
            maskc = sb("maskc", [128, 4, 33])
            diag16 = sb("diag16", [128, 16])
            notown = sb("notown", [128, 4, 32])
            identb = sb("identb", [128, 128], BF16)
            cmask = sb("cmask", [128, 128], BF16)
            cmaskT = sb("cmaskT", [128, 512], BF16)
            smask = sb("smask", [128, 2, 192], BF16)
            smaskT = sb("smaskT", [128, 2, 512], BF16)
            Q6 = sb("Q6", [128, 32, 512], BF16)
            K6 = sb("K6", [128, 2, 2, 8, 512], BF16)
            for t, n in ((wmod, "wmod0a"), (wq, "wq0"), (wg, "wg0"), (bg, "bg0"), (wo, "wo0"), (cb1, "cb1"),
                         (cw2k, "cw2k"), (cb2k, "cb2k"), (cw2v, "cw2v"), (cb2v, "cb2v"), (mck, "mck"), (mcv, "mcv"),
                         (rot, "rot0"), (maskc, "maskc"), (diag16, "diag16"), (notown, "notown"),
                         (identb, "identb"), (cmask, "cmask"), (cmaskT, "cmaskT"), (smask, "smask"),
                         (smaskT, "smaskT")):
                SP.dma(t[:], D[n], c_w)
            for x in range(4):
                SP.dma(K6[48:99, x % 2, x // 2, :, :], D["keyrows"][x // 2], c_w)
            for j in range(2):
                SP.dma(cw1[32 * j:32 * j + 8, :, :], D["cw1"][:, j], c_w)
                w = SP.dma(pos[32 * j:32 * j + 8, :, :], D["kvpos"][:, j], c_w)
            Xa = sb("X", [128, 8, 256])
            home.update(at=Xa, n=8)
            m_xa, x_done = {}, {}

            def load_x(b):
                m_xa[b] = SP.dma(Xa[:, 4 * (b % 2):4 * (b % 2) + 4, :], xin[:, 4 * b:4 * b + 4, :], c_xa[b % 2],
                                 x_done.get(b - 2))

            home["ready"] = lambda b: m_xa[b]
            h = sb("h", [128, 4, 256])
            hT = sb("hT", [128, 2, 512])
            qraw = sb("qraw", [128, 2, 512])
            rq = sb("rq", [128, 512])
            t1 = sb("t1", [128, 512])
            qsp = sb("qsp", [128, 3, 3, 512], BF16)
            kr = sb("kr", [40, 8, 512])
            v9 = sb("v9", [128, 2, 4, 8, 9])
            gt = sb("gt", [128, 2, 4, 96])
            bias1 = sb("bias1", [128, 2, 8])
            hk = sb("hk", [128, 256])
            ckt = sb("ckt", [128, 8, 32])
            ckb = sb("ckb", [128, 2, 16, 33])
            cvt = sb("cvt", [128, 8, 32])
            cs = sb("cs", [128, 32, 33])
            rv = cs[:].rearrange("p a b -> p (a b)")[:, 0:1024].rearrange("p (h g c) -> p h g c", h=8, g=4)
            eC = sb("eC", [128, 32, 32])
            kv = eC[:].rearrange("p a b -> p (a b)")[:, 0:512]
            eT = h[:].rearrange("p a (b c) -> p (a b) c", b=2)
            eM = sb("eM", [128, 32])
            z4 = sb("z4", [128, 4, 32])
            im = sb("im", [128, 8, 33])
            im2 = sb("im2", [128, 8, 33])
            imn = sb("imn", [128, 8, 32])
            m8 = sb("m8", [128, 8, 8])
            rp = sb("rp", [128, 8, 32])
            selb = sb("selb", [128, 256], BF16)
            selT = sb("selT", [128, 2, 2, 128], BF16)
            acc = sb("acc", [128, 2, 4, 256])
            mm = sb("mm", [128, 2, 2, 32])
            ms3 = sb("ms3", [128, 2, 3, 32], BF16)
            mr = sb("mr", [128, 2, 32])
            shT = sb("shT", [96, 2, 2, 128], BF16)
            PT = sb("PT", [128, 3, 512])
            OT = sb("OT", [128, 2, 512])
            zz = sb("zz", [128, 16])
            to = sb("to", [128, 128])
            oT = sb("oT", [128, 2, 128])
            tmp = sb("tmp", [128, 256])

            R1 = Ring([PS[:, i, :] for i in range(3)])
            RS = Ring([PS[:, 3 + i, :] for i in range(3)])
            RO = Ring([PS[:, 6 + i, :] for i in range(2)])
            LAG = 11

            V(lambda e: e.memset(OT[:], 0.0))
            V(lambda e: e.memset(im[:], -4000.0))
            V(lambda e: e.memset(cvt[:], 0.0))
            V(lambda e: e.memset(v9[:], 1.0))
            V(lambda e: e.memset(qsp[64:128, :, 2, :], 0.0))
            V(lambda e: e.tensor_scalar(mck[:], mck[:], S0, None, ALU.mult), w)
            for x in range(2):
                V(lambda e: e.tensor_tensor(
                    ckb[:, x, :, 0].rearrange("p (h g) -> p h g", g=4),
                    mck[:, 4 * x:4 * x + 4].unsqueeze(2).to_broadcast([128, 4, 4]),
                    diag16[:].rearrange("p (h g) -> p h g", g=4), ALU.mult))
            for j in range(2):
                n, p, f = R1.take()
                for t in range(16):
                    pe = T(lambda e: e.matmul(p[:, 0:8], cw1[32 * j:32 * j + 8, t, :], pos[32 * j:32 * j + 8, t, :],
                                              start=(t == 0), stop=(t == 15)), w, f)
                R1.free[n] = V(lambda e: e.tensor_scalar(bias1[:, j, :], p[:, 0:8], cb1[:, j:j + 1], None,
                                                         ALU.add), pe)
            V(lambda e: e.memset(Q6[64:128, :, :], 0.0))
            ready = [dict() for _ in range(8)]
            q6_free = [None] * 4
            k6_free = [None] * 8
            acc_free = [None] * 8
            m_sh, m_sel, m_exc = {}, {}, [None]
            sel_t, sh_t = [None] * 2, [None] * 2

            def split3(dst, src, rest, *marks):
                V(lambda e: e.tensor_copy(dst[0], src), *marks)
                V(lambda e: e.tensor_tensor(rest, src, dst[0], ALU.subtract))
                V(lambda e: e.tensor_copy(dst[1], rest))
                V(lambda e: e.tensor_tensor(rest, rest, dst[1], ALU.subtract))
                return V(lambda e: e.tensor_copy(dst[2], rest))

            def prepare(b):
                y = b % 2
                rd = ready[b]
                mod_rows(0, b, wmod, w, R1, mb=mb2[:, y, :, :])
                yield
                lv = layernorm(b, h, mb=mb2[:, y, :, :])
                yield
                hr = to_columns(h, hT, 0, R1, lv)
                yield

                def proj(c0, n_, *marks):
                    n, p, f = R1.take()
                    for k in range(2):
                        pe = T(lambda e: e.matmul(p[0:n_, :], wq[:, k, c0:c0 + n_], hT[:, k, :], start=(k == 0),
                                                  stop=(k == 1)), hr, w, f)
                    return n, p, pe

                n, p, pe = proj(512, 128)
                v = V(lambda e: e.tensor_copy(kv, p[:, :]), pe, c_k.mark())
                V(lambda e: e.tensor_tensor(rq[0:64, :], p[0:64, :], rot[0:64, 0, :], ALU.mult))
                R1.free[n] = V.mark()
                for j in range(2):
                    for hh in range(8):
                        r = 64 * j + 8 * hh
                        m_kr = SP.dma(kr[32 * j:32 * j + 8, hh, :], kv[r:r + 8, :], c_k, v)
                n, p, pe = proj(640, 64)
                R1.free[n] = V(lambda e: e.tensor_tensor(t1[0:64, :], p[0:64, :], rot[0:64, 1, :], ALU.mult), pe)
                V(lambda e: e.tensor_tensor(rq[0:64, :], rq[0:64, :], t1[0:64, :], ALU.add))
                yield
                m_ks = split3([qsp[0:64, s, 2, :] for s in range(3)], rq[0:64, :], t1[0:64, :], c_s.mark())
                yield
                for x in range(2):
                    n, p, pe = proj(128 * x, 128)
                    a = A(lambda e: e.activation(qraw[:, x, :], p[:, :], ACT.Copy), pe)
                    v = V(lambda e: e.tensor_tensor(rq[:], p[:, :], rot[:, 0, :], ALU.mult), a)
                    R1.free[n] = v
                    n, p, pe = proj(256 + 128 * x, 128)
                    R1.free[n] = V(lambda e: e.tensor_tensor(t1[:], p[:, :], rot[:, 1, :], ALU.mult), pe)
                    V(lambda e: e.tensor_tensor(rq[:], rq[:], t1[:], ALU.add))
                    yield
                    m_qs = split3([qsp[:, s, x, :] for s in range(3)], rq[:], t1[:])
                    yield
                rd["qraw"] = a
                for s in range(3):
                    SP.dma(D["scr"][s], qsp[:, s, :, :], c_s, m_qs, m_ks, [c.mark() for c in (*c_q, *c_k6)])
                rd["s"] = [c_s.mark(), c_k6[y].mark()]
                for j, s2 in enumerate((0, 1, 0, 2, 0, 1)):
                    for z in range(2):
                        rd["k6"] = SP.dma(K6[8 * j:8 * j + 8, y, z, :, :],
                                          D["scr"][s2, 0:64, 2, :].rearrange("(c d) t -> d c t", d=8), c_k6[y],
                                          rd["s"], k6_free[b - 2] if b >= 2 else None)
                yield
                n, p, f = R1.take()
                for i in range(4):
                    for k in range(2):
                        pe = T(lambda e: e.matmul(
                            p[:, 64 * i:64 * i + 64], hT[:, k, 128 * i:128 * i + 128], wq[:, k, 576:640],
                            start=(k == 0), stop=(k == 1)), f)
                rd["v9"] = R1.free[n] = V(lambda e: e.tensor_copy(
                    v9[:, y, :, :, :].rearrange("p i h d -> p (i h) d")[:, :, 0:8],
                    p[:, 0:256].rearrange("p (a d) -> p a d", d=8)), pe, k6_free[b - 2] if b >= 2 else None)
                yield
                n, p, f = R1.take()
                for i in range(4):
                    for k in range(2):
                        T(lambda e: e.matmul(
                            p[:, 96 * i:96 * i + 96], hT[:, k, 128 * i:128 * i + 128], wg[:, k, :],
                            start=(k == 0), stop=False), f)
                    pe = T(lambda e: e.matmul(p[:, 96 * i:96 * i + 96], ones[0:1, :], bg[0:1, :],
                                              start=False, stop=True), v_ones)
                rd["gt"] = R1.free[n] = A(lambda e: e.activation(gt[:, y, :, :].rearrange("p a b -> p (a b)"),
                                                                 p[:, 0:384], ACT.Sigmoid), pe, V.mark())
                yield
                for j in range(2):
                    n, p, f = R1.take()
                    for t in range(16):
                        pe = T(lambda e: e.matmul(
                            p[:, 0:256], cw1[32 * j:32 * j + 8, t, :],
                            kr[32 * j:32 * j + 8, :, :].rearrange("d h (c t) -> d h c t", t=16)[:, :, :, t],
                            start=(t == 0), stop=(t == 15)), m_kr, f)
                    V(lambda e: e.tensor_tensor(
                        hk[:].rearrange("p (h c) -> p h c", h=8), p[:, 0:256].rearrange("p (h c) -> p h c", h=8),
                        bias1[:, j, :].unsqueeze(2).to_broadcast([128, 8, 32]), ALU.add), pe)
                    if j == 0:
                        v = R1.free[n] = V(lambda e: e.tensor_scalar(hk[:], hk[:], 0.0, None, ALU.max))
                        n, p, f = R1.take()
                        pe = T(lambda e: e.matmul(p[:, 0:256], cw2k[:], hk[:], start=True, stop=True), v, f)
                        R1.free[n] = V(lambda e: e.tensor_scalar(
                            ckt[:].rearrange("p h c -> p (h c)"), p[:, 0:256], cb2k[:, 0:1], S0,
                            ALU.add, ALU.mult), pe)
                        yield
                        for x in range(2):
                            for g in range(4):
                                rd["ck"] = V(lambda e: e.tensor_tensor(
                                    ckb[:, x, g:16:4, 1:33], ckt[:, 4 * x:4 * x + 4, :],
                                    diag16[:, g:16:4].unsqueeze(2).to_broadcast([128, 4, 32]), ALU.mult))
                    else:
                        for g in range(4):
                            v = V(lambda e: e.tensor_scalar(
                                rv[:, :, g, :], hk[:].rearrange("p (h c) -> p h c", h=8), 0.0, None, ALU.max))
                        R1.free[n] = v
                        yield
                        n, p, f = R1.take()
                        for hh in range(8):
                            pe = T(lambda e: e.matmul(
                                p[:, 8 * hh:8 * hh + 8], rv[:, hh, :, :].rearrange("p g c -> p (g c)"), cw2v[:],
                                start=True, stop=True), v, f)
                        for g in range(4):
                            r = slice(32 * g, 32 * g + 32)
                            rd["cv"] = R1.free[n] = V(lambda e: e.tensor_tensor(
                                cvt[r, :, 8 * g:8 * g + 8], p[r, 0:64].rearrange("p (h d) -> p h d", h=8),
                                cb2v[r, :].unsqueeze(1).to_broadcast([32, 8, 8]), ALU.add), pe)
                yield

            def compressed(b, i):
                rd = ready[b]
                y = b % 2
                ac = acc[:, y, i, :]
                qc = slice(128 * i, 128 * i + 128)
                SP.wait(c_q[i % 2].mark())
                for j, s in enumerate((0, 0, 1, 0, 2, 1)):
                    for x in range(2):
                        rd["q6", i] = SP.dma(Q6[8 * j:8 * j + 8, 16 * x:16 * x + 16, qc],
                                             D["scr"][s, :, x, qc].rearrange("(c d) t -> d c t", d=8),
                                             c_q[i % 2], rd["s"], q6_free[i])
                for q4 in range(4):
                    n, p, f = R1.take()
                    x, c = q4 // 2, 8 * (q4 % 2)
                    pe = T(lambda e: e.matmul(p[:, 0:264], qraw[:, x, qc],
                                              ckb[:, x, c:c + 8, :].rearrange("p a b -> p (a b)"),
                                              start=True, stop=True), rd["ck"], rd["qraw"], f)
                    R1.free[n] = V(lambda e: e.tensor_tensor(
                        cs[:, 8 * q4:8 * q4 + 8, :],
                        p[:, 0:264].rearrange("p (u j) -> p u j", u=8),
                        maskc[:, i, :].unsqueeze(1).to_broadcast([128, 8, 33]), ALU.add), pe, m_exc[0])
                    if q4 == 1:
                        yield
                yield
                V(lambda e: e.tensor_reduce(z4[:, 0, :], cs[:], AX, ALU.max))
                V(lambda e: e.tensor_reduce(im[:, :, 1:33], cs[:].rearrange("p (h g) j -> p h j g", g=4)
                                            [:, :, 1:33, :], AX, ALU.add))
                v = V(lambda e: e.tensor_tensor(cs[:], cs[:], z4[:, 0, :].unsqueeze(2).to_broadcast([128, 32, 33]),
                                                ALU.subtract))
                V(lambda e: e.tensor_reduce(z4[:, 1, 0:8], im[:], AX, ALU.max))
                v2 = V(lambda e: e.tensor_tensor(im2[:], im[:], z4[:, 1, 0:8].unsqueeze(2)
                                                 .to_broadcast([128, 8, 33]), ALU.subtract))
                a2 = A(lambda e: e.activation(im2[:], im2[:], ACT.Exp, scale=0.25), v2)
                A(lambda e: e.activation(eM[:], cs[:, :, 0], ACT.Exp), v)
                a = m_exc[0] = A(lambda e: e.activation(eC[:], cs[:, :, 1:33], ACT.Exp), v)
                yield
                V(lambda e: e.tensor_reduce(z4[:, 1, 8:16], im2[:], AX, ALU.add), a2)
                V(lambda e: e.reciprocal(z4[:, 1, 16:24], z4[:, 1, 8:16]))
                V(lambda e: e.tensor_tensor(imn[:], im2[:, :, 1:33], z4[:, 1, 16:24].unsqueeze(2)
                                            .to_broadcast([128, 8, 32]), ALU.mult))
                for hh in range(8):
                    V(lambda e: e.max(m8[:, hh, :], imn[:, hh, :]))
                yield
                for hh in range(8):
                    V(lambda e: e.match_replace(rp[:, hh, :], m8[:, hh, :], imn[:, hh, :], -1.0))
                V(lambda e: e.tensor_scalar(rp[:], rp[:], 0.0, NEG, ALU.is_ge, ALU.mult))
                V(lambda e: e.tensor_scalar(imn[:], imn[:], 1e-10, NEG, ALU.is_le, ALU.mult))
                V(lambda e: e.tensor_tensor(rp[:], rp[:], imn[:], ALU.min))
                v = V(lambda e: e.tensor_tensor(selb[:].rearrange("p (h c) -> p h c", h=8), rp[:],
                                                notown[:, i, :].unsqueeze(1).to_broadcast([128, 8, 32]),
                                                ALU.mult))
                yield
                n, p, f = R1.take()
                pb = p.bitcast(BF16)
                for u in range(2):
                    pe = T(lambda e: e.transpose(pb[:, 128 * u:128 * u + 128], selb[:, 128 * u:128 * u + 128],
                                                 identb[:]), v, f)
                v = R1.free[n] = V(lambda e: e.tensor_copy(
                    selT[:, i % 2, :, :].rearrange("p a b -> p (a b)"), pb[:, 0:256]), pe, sel_t[i % 2])
                for hh in range(8):
                    r = 32 * (hh % 4)
                    for g in range(4):
                        m_sel[b, i] = sel_t[i % 2] = SP.dma(Q6[48:80, 4 * hh + g, qc], selT[r:r + 32, i % 2, hh // 4, :],
                                          c_m[i % 2], v, q6_free[i])
                yield
                for half in range(2):
                    n, p, f = R1.take()
                    for u in range(4):
                        hh = 4 * half + u
                        pe = T(lambda e: e.transpose(
                            p[:, 128 * u:128 * u + 128],
                            eC[:, 4 * hh:4 * hh + 4, :].rearrange("p g c -> p (g c)"), ident[:]), a, f)
                    a3 = R1.free[n] = A(lambda e: e.activation(
                        eT[:, 4 * half:4 * half + 4, :].rearrange("p a b -> p (a b)"), p[:, :], ACT.Copy), pe)
                n, p, f = R1.take()
                for hh in range(8):
                    pe = T(lambda e: e.matmul(p[:, 32 * hh:32 * hh + 32], eT[:, hh, :], cvt[:, hh, :],
                                              start=True, stop=True), a3, rd["cv"], f)
                V(lambda e: e.tensor_reduce(z4[:, 2, :], eC[:], AX, ALU.add), a)
                V(lambda e: e.tensor_tensor(z4[:, 2, :], z4[:, 2, :], eM[:], ALU.add))
                V(lambda e: e.reciprocal(z4[:, 3, :], z4[:, 2, :]))
                V(lambda e: e.tensor_tensor(z4[:, 3, :], z4[:, 3, :], gt[:, y, i, 0:96:3], ALU.mult), rd["gt"])
                V(lambda e: e.tensor_tensor(
                    ac.rearrange("p (h g d) -> p h g d", h=8, g=4),
                    eM[:].rearrange("p (h g) -> p h g", g=4).unsqueeze(3).to_broadcast([128, 8, 4, 8]),
                    mcv[:].unsqueeze(2).to_broadcast([128, 8, 4, 8]), ALU.mult), acc_free[b - 2] if b >= 2 else None)
                m_exc[0] = [m_exc[0], V.mark()]
                R1.free[n] = V(lambda e: e.tensor_tensor(ac, ac, p[:, 0:256], ALU.add), pe)
                V(lambda e: e.tensor_tensor(
                    ac.rearrange("p (a d) -> p a d", d=8), ac.rearrange("p (a d) -> p a d", d=8),
                    z4[:, 3, :].unsqueeze(2).to_broadcast([128, 32, 8]), ALU.mult))

            def maxima(b, u):
                i, hh = u // 8, u % 8
                y = b % 2
                qc = slice(128 * i, 128 * i + 128)
                nk = 128 * (i + 1)
                for g in range(4):
                    c = 4 * hh + g
                    n, p, f = R1.take()
                    T(lambda e: e.matmul(p[:, 0:nk], Q6[0:80, c, qc], K6[0:80, y, 0, hh, 0:nk],
                                         start=True, stop=False), m_sel[b, i], ready[b]["q6", i], ready[b]["k6"],
                      w, f)
                    pe = T(lambda e: e.matmul(p[:, nk - 128:nk], identb[:], cmask[:], start=False, stop=True))
                    R1.free[n] = V(lambda e: e.tensor_reduce(mm[:, i % 2, 0, c:c + 1], p[:, 0:nk], AX, ALU.max),
                                   pe)
                lo = 64 if i else 128
                for g2 in range(2):
                    n, p, f = R1.take()
                    k0 = 0 if i else 64
                    n_ = 192 - k0
                    for g in range(2):
                        c = 4 * hh + 2 * g2 + g
                        o = n_ * g
                        T(lambda e: e.matmul(p[:, o:o + n_], Q6[0:96, c, qc], K6[0:96, y, 1, hh, nk - n_:nk],
                                             start=True, stop=False), f)
                        pe = T(lambda e: e.matmul(p[:, o:o + n_], identb[:], smask[:, 0, k0:192],
                                                  start=False, stop=True))
                    c = 4 * hh + 2 * g2
                    R1.free[n] = V(lambda e: e.tensor_reduce(
                        mm[:, i % 2, 1, c:c + 2], p[:, 0:2 * n_].rearrange("p (g k) -> p g k", g=2), AX,
                        ALU.max), pe)
                if hh == 7:
                    for kind in range(2):
                        V(lambda e: e.tensor_scalar(mr[:, 0, :], mm[:, i % 2, kind, :], -1.0, None, ALU.mult))
                        v = split3([ms3[:, kind, s, :] for s in range(3)], mr[:, 0, :], mr[:, 1, :])
                        n, p, f = R1.take()
                        pb = p.bitcast(BF16)
                        pe = T(lambda e: e.transpose(
                            pb[0:96, 0:128], ms3[:, kind, :, :].rearrange("p a b -> p (a b)"), identb[:]), v, f)
                        v = R1.free[n] = V(lambda e: e.tensor_copy(shT[:, i % 2, kind, :], pb[0:96, 0:128]), pe,
                                           sh_t[i % 2])
                        for s in range(3):
                            row = (80, 96)[kind] + s
                            m_sh[b, i] = SP.dma(Q6[row:row + 1, :, qc], shT[32 * s:32 * s + 32, i % 2, kind, :],
                                             c_h[i % 2], v, q6_free[i])
                    sh_t[i % 2] = m_sh[b, i]

            hist2 = []

            pend, last_pv = [], []
            ot_w, ot_free = {}, {}

            def weigh(b, u):
                i, hh = u // 8, u % 8
                y = b % 2
                qc = slice(128 * i, 128 * i + 128)
                for kind in range(2):
                    kts = list(range(i + 1)) if kind == 0 else list(range(max(i - 1, 0), i + 1))
                    bank = RO.take()
                    for kt in kts:
                        kc = slice(128 * kt, 128 * kt + 128)
                        n, p, f = RS.take()
                        rows = (83, 99)[kind]
                        masked = kind == 1 or kt == i
                        pe = T(lambda e: e.matmul(p[:, :], K6[0:rows, y, kind, hh, kc],
                                                  Q6[0:rows, 4 * hh:4 * hh + 4, qc],
                                                  start=True, stop=not masked), m_sh[b, i], f)
                        if masked:
                            mk = smaskT[:, kt - i + 1, :] if kind else cmaskT[:]
                            pe = T(lambda e: e.matmul(p[:, :], identb[:], mk, start=False, stop=True))
                        if len(pend) == 2:
                            times(*pend.pop(0))
                        r = len(last_pv) + len(pend)
                        a = RS.free[n] = A(lambda e: e.activation(PT[:, r % 3, :], p[:, :], ACT.Exp, scale=S0), pe,
                                           last_pv[r - 3] if r >= 3 else None)
                        pend.append((b, i, hh, kind, kt, kt == kts[0], kt == kts[-1], r % 3, a, bank))

            def times(b, i, hh, kind, kt, first, last, r, a, bank):
                no, po, fo = bank
                m = T(lambda e: e.matmul(po[0:9, :], v9[:, b % 2, kt, hh, :], PT[:, r, :], start=first, stop=last),
                      a, ready[b]["v9"], fo)
                last_pv.append(m)
                if not last:
                    return
                r = 32 * (hh % 4)
                RO.free[no] = ot_w[kind] = A(lambda e: e.activation(OT[r:r + 9, kind, :], po[0:9, :], ACT.Copy), m,
                                             ot_free.get(kind))
                if hh % 4 == 3:
                    weighed(b, i, hh // 4, kind)

            def weighed(b, i, hf, kind):
                y = b % 2
                n, p, f = R1.take()
                for g in range(4):
                    pe = T(lambda e: e.transpose(p[:, 128 * g:128 * g + 128],
                                                 OT[:, kind, 128 * g:128 * g + 128], ident[:]), ot_w[kind], f)
                ot_free[kind] = pe
                pv = p[:, :].rearrange("p (g h j) -> p g h j", g=4, h=4)
                gv = gt[:, y, i, 48 * hf:48 * hf + 48].rearrange("p (h g s) -> p g h s", g=4, s=3)
                zv = zz[:].rearrange("p (g h) -> p g h", g=4)
                V(lambda e: e.reciprocal(zv, pv[:, :, :, 8]), pe)
                V(lambda e: e.tensor_tensor(zv, zv, gv[:, :, :, 1 + kind], ALU.mult))
                tv = to[:].rearrange("p (g h d) -> p g h d", g=4, h=4)
                V(lambda e: e.tensor_tensor(tv, pv[:, :, :, 0:8], zv.unsqueeze(3).to_broadcast([128, 4, 4, 8]),
                                            ALU.mult))
                av = acc[:, y, i, 128 * hf:128 * hf + 128].rearrange("p (h g d) -> p g h d", h=4, g=4)
                v = R1.free[n] = V(lambda e: e.tensor_tensor(av, av, tv, ALU.add))
                if hf == 1 and kind == 1:
                    finish(b, i, v)

            def finish(b, i, v):
                n, p, f = R1.take()
                for k in range(2):
                    pe = T(lambda e: e.transpose(p[:, 128 * k:128 * k + 128],
                                                 acc[:, b % 2, i, 128 * k:128 * k + 128], ident[:]), v, f)
                v = R1.free[n] = V(lambda e: e.tensor_copy(oT[:].rearrange("p a b -> p (a b)"), p[:, 0:256]), pe)
                n2, p2, f2 = R1.take()
                for k in range(2):
                    pe = T(lambda e: e.matmul(p2[:, 0:256], oT[:, k, :], wo[:, k, :], start=(k == 0),
                                              stop=(k == 1)), v, f2)
                R1.free[n2] = add_gated(4 * b + i, p2[:, 0:256], pe, tmp[:], mb=mb2[:, b % 2, :, :])

            def chain(*gens):
                for g in gens:
                    yield from g

            def advance(gen, k):
                for _ in range(k):
                    next(gen, None)

            load_x(0)
            load_x(1)
            for _ in chain(prepare(0), compressed(0, 0)):
                pass
            for b in range(8):
                plan = [(compressed(b, 1), 0, 7), (compressed(b, 2), 6, 13), (compressed(b, 3), 12, 19)]
                if b < 7:
                    plan.append((chain(prepare(b + 1), compressed(b + 1, 0)), 20, 32))
                for u in range(32 + (LAG if b == 7 else 0)):
                    if u < 32:
                        maxima(b, u)
                    for c, v in ((b, u - LAG), (b - 1, u + 32 - LAG)):
                        if c >= 0 and 0 <= v < 32:
                            weigh(c, v)
                            if v % 8 == 7:
                                q6_free[v // 8] = T.mark()
                            if v == 31:
                                while pend:
                                    times(*pend.pop(0))
                                k6_free[c] = [T.mark(), V.mark()]
                                acc_free[c] = T.mark()
                                x_done[c] = SP.dma(xout[:, 4 * c:4 * c + 4, :],
                                                   Xa[:, 4 * (c % 2):4 * (c % 2) + 4, :], c_o, V.mark())
                                if c + 2 < 8:
                                    load_x(c + 2)
                    for gen, first, last in plan:
                        if first <= u < last:
                            advance(gen, 3 if first == 20 else 2)
                        if u == last - 1:
                            advance(gen, 100)

        def phase_b(ctx):
            def sb(n, shape, dt=F32):
                return sbt(ctx, "b_" + n, shape, dt)

            wmod = sb("wmod", [128, 2, 768])
            iota = sb("iota", [128, 32])
            ti = sb("ti", [128, 16, 4], I32)
            tx = sb("tx", [128, 16, 4])
            tw = sb("tw", [128, 16, 4])
            rw = sb("rw", [128, 16, 32])
            oh = sb("oh", [128, 16, 32])
            SP.dma(wmod[:], D["wmod0b"], c_w)
            SP.dma(iota[:], D["iota"], c_w)
            SP.dma(ti[:], D["tidx"].rearrange("(i p) k -> p i k", p=128), c_w)
            w = SP.dma(tw[:], D["tw"].rearrange("(i p) k -> p i k", p=128), c_w)
            h = sb("h", [128, 4, 256])
            hT = sb("hT", [128, 2, 2048])
            acc = sb("acc", [128, 16, 256])
            gb = sb("gb", [128, 4, 256])
            we = sb("we", [128, 3, 768])
            sg = sb("sg", [128, 3, 512])
            hm = sb("hm", [128, 3, 512])
            tmp = sb("tmp", [128, 256])
            wfree = [None] * 3
            wm = {}

            def load(ex):
                r = ex % 3
                wm[ex] = SP.dma(we[:, r, :], D["exp0"][ex], c_e[r], wfree[r])

            for ex in range(3):
                load(ex)
            V(lambda e: e.memset(acc[:], 0.0))
            V(lambda e: e.tensor_copy(tx[:], ti[:]), w)
            for k in range(4):
                V(lambda e, k=k: e.tensor_tensor(oh[:], iota[:].unsqueeze(1).to_broadcast([128, 16, 32]),
                                                 tx[:, :, k:k + 1].to_broadcast([128, 16, 32]), ALU.is_equal))
                d = rw if k == 0 else oh
                V(lambda e, k=k, d=d: e.tensor_tensor(d[:], oh[:], tw[:, :, k:k + 1].to_broadcast([128, 16, 32]),
                                                      ALU.mult))
                if k:
                    V(lambda e: e.tensor_tensor(rw[:], rw[:], oh[:], ALU.add))
            RG = Ring([PS[:, i, :] for i in range(4)])
            RD = Ring([PS[:, 4 + i, :] for i in range(4)])
            for b in range(4):
                mod_rows(0, b, wmod, w, RG)
                V(lambda e, b=b: e.tensor_copy(gb[:, b, :], mb[:, 2, :]))
                lv = layernorm(b, h, T.mark())
                hr = to_columns(h, hT, 512 * b, RG, lv)
            jobs = [(ex, c) for ex in range(32) for c in range(4)]
            st = [dict() for _ in jobs]

            def up(t):
                ex, c = jobs[t]
                r, r3 = ex % 3, t % 3
                ps = []
                for o in (0, 128):
                    n, p, f = RG.take()
                    for k in range(2):
                        pe = T(lambda e, k=k, o=o, p=p: e.matmul(
                            p[:, :], we[:, r, 256 * k + o:256 * k + o + 128], hT[:, k, 512 * c:512 * c + 512],
                            start=(k == 0), stop=(k == 1)), hr, wm[ex], f)
                    ps.append((n, p, pe))
                (n1, p1, e1), (n2, p2, e2) = ps
                a = RG.free[n1] = A(lambda e: e.activation(sg[:, r3, :], p1[:, :], ACT.Silu), e1,
                                    st[t - 3]["hm"] if t >= 3 else None)
                st[t]["hm"] = RG.free[n2] = V(lambda e: e.tensor_tensor(hm[:, r3, :], sg[:, r3, :], p2[:, :], ALU.mult),
                                              a, e2, st[t - 3]["pe"] if t >= 3 else None)

            def down(t):
                ex, c = jobs[t]
                r, r3 = ex % 3, t % 3
                for i in range(4):
                    n, p, f = RD.take()
                    pe = T(lambda e, i=i, p=p: e.matmul(p[:, 0:256], hm[:, r3, 128 * i:128 * i + 128],
                                                        we[:, r, 512:768], start=True, stop=True), st[t]["hm"], f)
                    g = 4 * c + i
                    RD.free[n] = V(lambda e, p=p, g=g: e.scalar_tensor_tensor(
                        acc[:, g, :], p[:, 0:256], rw[:, g, ex:ex + 1], acc[:, g, :], ALU.mult, ALU.add), pe)
                st[t]["pe"] = pe
                if c == 3:
                    wfree[r] = pe
                    if ex + 3 < 32:
                        load(ex + 3)

            for t in range(len(jobs) + 1):
                if t < len(jobs):
                    up(t)
                if t:
                    down(t - 1)
            for b in range(4):
                for i in range(4):
                    V(lambda e, b=b, i=i: e.tensor_tensor(tmp[:], acc[:, 4 * b + i, :], gb[:, b, :], ALU.mult))
                    V(lambda e, b=b, i=i: e.tensor_tensor(X(4 * b + i), X(4 * b + i), tmp[:], ALU.add))

        def phase_c(ctx):
            def sb(n, shape, dt=F32):
                return sbt(ctx, "c_" + n, shape, dt)

            wmod = sb("wmod", [128, 2, 768])
            wa = sb("wa", [128, 2, 768])
            ba = sb("ba", [128, 4])
            bv = sb("bv", [1, 256])
            wp = sb("wp", [128, 2, 256])
            bp = sb("bp", [1, 256])
            cg = sb("cg", [128, 1])
            lw = sb("lw", [128, 4])
            for t, n in ((wmod, "wmod1a"), (wa, "wa1"), (ba, "ba1"), (bv, "bv1"), (wp, "wp1"), (bp, "bp1"), (cg, "cg1")):
                SP.dma(t[:], D[n], c_w)
            SP.dma(lw[:, 0:1], D["cw0"], c_w)
            w = SP.dma(lw[:, 1:2], D["cw1c"], c_w)
            v = V(lambda e: e.scalar_tensor_tensor(lw[:, 2:3], lw[:, 1:2], 0.5, lw[:, 0:1], ALU.mult, ALU.add), w)
            m_lw = A(lambda e: e.activation(lw[:, 3:4], lw[:, 2:3], ACT.Sigmoid), v)
            h = sb("h", [128, 4, 256])
            hT = sb("hT", [128, 2, 512])
            QK = sb("QK", [128, 4, 512])
            Vt = sb("Vt", [128, 4, 256])
            P = sb("P", [128, 4, 512])
            PT = sb("PT", [128, 4, 512])
            tc = sb("tc", [128, 512])
            z = sb("z", [128, 4, 4])
            o = sb("o", [128, 4, 256])
            oT = sb("oT", [128, 2, 512])
            tmp = sb("tmp", [128, 256])
            R = Ring([PS[:, i, :] for i in range(8)])

            def softmax(i, n, p, pe, ta):
                V(lambda e: e.tensor_reduce(z[:, 0, i:i + 1], p[:, :], AX, ALU.max), pe)
                v = V(lambda e: e.tensor_scalar(z[:, 1, i:i + 1], z[:, 0, i:i + 1], -S1, None, ALU.mult))
                R.free[n] = A(lambda e: e.activation(P[:, i, :], p[:, :], ACT.Exp, bias=z[:, 1, i:i + 1], scale=S1,
                                                     accum_out=z[:, 2, i:i + 1]), v, ta)
                return R.free[n]

            def turn_all(ready):
                ms = []
                old = T.mark()
                for j in range(4):
                    n, p, f = R.take()
                    for i in range(4):
                        pe = T(lambda e, i=i, j=j, p=p: e.transpose(p[:, 128 * i:128 * i + 128],
                                                                    P[:, i, 128 * j:128 * j + 128], ident[:]),
                               ready, f)
                    m = R.free[n] = evac((V, A)[j % 2], PT[:, j, :], p[:, :], pe, old)
                    ms.append(m)
                return ms

            for b in range(8):
                mod_rows(1, b, wmod, w, R)
                lv = layernorm(b, h, T.mark())
                hr = to_columns(h, hT, 0, R, lv, T.mark())
                old = T.mark()
                for m in range(4):
                    n, p, f = R.take()
                    for k in range(2):
                        pe = T(lambda e, k=k, m=m, p=p: e.matmul(p[:, :], wa[:, k, 128 * m:128 * m + 128], hT[:, k, :],
                                                                 start=(k == 0), stop=(k == 1)), hr, w, f)
                    m_qk = R.free[n] = V(lambda e, m=m, p=p: e.tensor_scalar(QK[:, m, :], p[:, :], ba[:, m:m + 1], None,
                                                                             ALU.add), pe)
                for i in range(4):
                    n, p, f = R.take()
                    for k in range(2):
                        T(lambda e, k=k, i=i, p=p: e.matmul(p[:, 0:256], hT[:, k, 128 * i:128 * i + 128],
                                                            wa[:, k, 512:768], start=(k == 0), stop=False), f)
                    pe = T(lambda e, p=p: e.matmul(p[:, 0:256], ones[0:1, :], bv[0:1, :], start=False, stop=True),
                           v_ones)
                    m_v = R.free[n] = V(lambda e, i=i, p=p: e.tensor_copy(Vt[:, i, :], p[:, 0:256]), pe)
                old = T.mark()
                ex = []
                for i in range(4):
                    n, p, f = R.take()
                    pe = T(lambda e, i=i, p=p: e.matmul(p[:, :], QK[:, 0, 128 * i:128 * i + 128], QK[:, 2, :],
                                                        start=True, stop=True), m_qk, f)
                    ex.append(softmax(i, n, p, pe, old))
                for i in range(4):
                    V(lambda e, i=i: e.reciprocal(z[:, 3, i:i + 1], z[:, 2, i:i + 1]), ex[i])
                    v = V(lambda e, i=i: e.tensor_scalar(P[:, i, :], P[:, i, :], z[:, 3, i:i + 1], None, ALU.mult))
                pt = turn_all(v)
                n, p, f = R.take()
                for j in range(4):
                    pe = T(lambda e, j=j, p=p: e.matmul(p[:, :], Vt[:, j, 0:128], PT[:, j, :], start=(j == 0),
                                                        stop=(j == 3)), pt, m_v, f)
                a = R.free[n] = A(lambda e, p=p: e.activation(tc[:], p[:, :], ACT.Tanh, scale=cg[:, 0:1]), pe,
                                  V.mark(), T.mark())
                v = V(lambda e: e.tensor_scalar(tc[:], tc[:], lw[:, 3:4], None, ALU.mult), a, m_lw)
                old = T.mark()
                ex = []
                for i in range(4):
                    n, p, f = R.take()
                    qc = slice(128 * i, 128 * i + 128)
                    T(lambda e, qc=qc, p=p: e.matmul(p[:, :], QK[:, 0, qc], QK[:, 2, :], start=True, stop=False), f)
                    T(lambda e, qc=qc, p=p: e.matmul(p[:, :], QK[:, 1, qc], QK[:, 3, :], start=False, stop=False))
                    pe = T(lambda e, qc=qc, p=p: e.matmul(p[:, :], tc[:, qc], QK[:, 2, :], start=False, stop=True), v)
                    ex.append(softmax(i, n, p, pe, old))
                pt = turn_all(ex)
                for i in range(4):
                    n, p, f = R.take()
                    for j in range(4):
                        pe = T(lambda e, j=j, i=i, p=p: e.matmul(p[:, 0:256], PT[:, j, 128 * i:128 * i + 128],
                                                                 Vt[:, j, :], start=(j == 0), stop=(j == 3)), pt, f)
                    V(lambda e, i=i: e.reciprocal(z[:, 3, i:i + 1], z[:, 2, i:i + 1]))
                    v = R.free[n] = V(lambda e, i=i, p=p: e.tensor_scalar(o[:, i, :], p[:, 0:256], z[:, 3, i:i + 1],
                                                                          None, ALU.mult), pe)
                om = to_columns(o, oT, 0, R, v, T.mark())
                for i in range(4):
                    n, p, f = R.take()
                    for k in range(2):
                        T(lambda e, k=k, i=i, p=p: e.matmul(p[:, 0:256], oT[:, k, 128 * i:128 * i + 128], wp[:, k, :],
                                                            start=(k == 0), stop=False), om, f)
                    pe = T(lambda e, p=p: e.matmul(p[:, 0:256], ones[0:1, :], bp[0:1, :], start=False, stop=True))
                    R.free[n] = add_gated(4 * b + i, p[:, 0:256], pe, tmp[:])

        def phase_d(ctx, HT, RW):
            def sb(n, shape, dt=F32):
                return sbt(ctx, "d_" + n, shape, dt)

            wmod = sb("wmod", [128, 2, 768])
            lnw = sb("lnw", [128, 2, 256])
            rot = sb("rot", [128, 3, 512])
            causal = sb("causal", [128, 512])
            iota = sb("iota", [128, 16])
            wv = sb("wv", [128, 2, 512])
            wo = sb("wo", [128, 16, 256])
            wg = sb("wg", [128, 2, 16])
            for t, n in ((lnw, "lnw"), (rot, "rot1"), (causal, "causal"), (wv, "wv1"), (wo, "wo1"), (wg, "wgr")):
                SP.dma(t[:], D[n], c_w)
            SP.dma(iota[:], D["iota"][:, 0:16], c_w)
            w = SP.dma(wmod[:], D["wmod1b"], c_w)
            wh = sb("wh", [128, 2, 2, 768])
            y2 = sb("y", [128, 2, 4, 256])
            hT2 = sb("hT", [128, 2, 2, 512])
            qs = sb("qs", [128, 2, 4, 512])
            ks = sb("ks", [128, 2, 512])
            t1 = sb("t1", [128, 2, 512])
            h = t1[:].rearrange("p a (b c) -> p (a b) c", b=2)
            vt = sb("vt", [128, 4, 512])
            fm = sb("fm", [128, 3, 512])
            ef = sb("ef", [128, 4, 512])
            tf = sb("tf", [128, 2, 4, 4, 128])
            bs = sb("bs", [128, 4])
            zz = sb("zz", [128, 4, 4])
            zr = sb("zr", [128, 4, 4])
            oT = sb("oT", [128, 2, 2, 128])
            tmp = sb("tmp", [128, 256])
            rt = sb("rt", [128, 6, 16])
            ri = sb("ri", [128, 8], U32)
            RS = Ring([PS[:, i, :] for i in (0, 1, 5)])
            RF = Ring([PS[:, 2 + i, :] for i in range(2)])
            RO = Ring([PS[0:64, 4 + i, :] for i in range(1)])
            Y = [PS[:, 6, 0:256], PS[:, 6, 256:512], PS[:, 7, 0:256], PS[:, 7, 256:512]]
            y_free = None
            n_w = 0
            whfree = [None, None]
            whm = {}

            def load(k):
                whm[k] = SP.dma(wh[:, k % 2, :, :], D["wh1"][k % 8], c_e[k % 2], whfree[k % 2])

            load(0)
            load(1)
            qk_free = [None, None]
            z_free = [None] * 4
            oT_free = [None, None]
            hist = []

            def past(t, key):
                return hist[t][key] if t >= 0 else None

            ready = [dict() for _ in range(8)]

            def before(b):
                rd, c = ready[b], b % 2
                mod_rows(1, b, wmod, w, RS, mb=mb2[:, c, :, :])
                yield
                layernorm(b, y2[:, c, :, :], mb=mb2[:, c, :, :])
                yield
                lv = rmsnorm(y2[:, c, :, :], lnw[:, 0, :], h, tmp[:], T.mark())
                rd["hT"] = to_columns(h, hT2[:, c, :, :], 0, RS, lv)
                yield

            def values(b):
                rd, c = ready[b], b % 2
                for i in range(4):
                    n, p, f = RS.take()
                    for k in range(2):
                        pe = T(lambda e: e.matmul(p[:, :], hT2[:, c, k, 128 * i:128 * i + 128], wv[:, k, :],
                                                  start=(k == 0), stop=(k == 1)), rd["hT"], w, f)
                    rd["v"] = RS.free[n] = V(lambda e: e.tensor_copy(vt[:, i, :], p[:, :]), pe)
                return rd["v"]

            def after(b):
                c = b % 2
                y = y2[:, c, :, :]
                lv = rmsnorm(y, lnw[:, 1, :], h, tmp[:], T.mark())
                hw = to_columns(h, HT, 512 * b, RS, lv)
                yield
                for i in range(4):
                    V(lambda e: e.tensor_tensor(tmp[:], y[:, i, :], mb2[:, c, 2, :], ALU.mult))
                    V(lambda e: e.tensor_tensor(X(4 * b + i), X(4 * b + i), tmp[:], ALU.add))
                    n, p, f = RS.take()
                    for k in range(2):
                        pe = T(lambda e, k=k, i=i, b=b, p=p: e.matmul(
                            p[:, 0:16], HT[:, k, 512 * b + 128 * i:512 * b + 128 * i + 128], wg[:, k, :],
                            start=(k == 0), stop=(k == 1)), hw, w, f)
                    RS.free[n] = V(lambda e, p=p: e.tensor_copy(rt[:, 0, :], p[:, 0:16]), pe)
                    V(lambda e: e.max(rt[:, 1, 0:8], rt[:, 0, :]))
                    V(lambda e: e.max_index(ri[:], rt[:, 1, 0:8], rt[:, 0, :]))
                    V(lambda e: e.tensor_copy(rt[:, 2, 0:8], ri[:]))
                    v = V(lambda e: e.tensor_scalar(rt[:, 1, 8:9], rt[:, 1, 0:1], -1.0, None, ALU.mult))
                    a = A(lambda e: e.activation(rt[:, 3, 0:4], rt[:, 1, 0:4], ACT.Exp, bias=rt[:, 1, 8:9],
                                                 accum_out=rt[:, 3, 4:5]), v)
                    V(lambda e: e.reciprocal(rt[:, 3, 5:6], rt[:, 3, 4:5]), a)
                    V(lambda e: e.tensor_scalar(rt[:, 3, 8:12], rt[:, 3, 0:4], rt[:, 3, 5:6], None, ALU.mult))
                    for k in range(4):
                        d = RW[:, 4 * b + i, :] if k == 0 else rt[:, 4, :]
                        V(lambda e, k=k, d=d: e.tensor_scalar(d, iota[:], rt[:, 2, k:k + 1], rt[:, 3, 8 + k:9 + k],
                                                              ALU.is_equal, ALU.mult))
                        if k:
                            V(lambda e, b=b, i=i: e.tensor_tensor(RW[:, 4 * b + i, :], RW[:, 4 * b + i, :],
                                                                  rt[:, 4, :], ALU.add))
                    yield

            for _ in before(0):
                pass
            behind = iter(())
            for b in range(8):
                hr, m_v = ready[b]["hT"], values(b)
                hT = hT2[:, b % 2, :, :]
                ahead = before(b + 1) if b < 7 else iter(())
                m_q = {}

                def project(hh):
                    kk = 8 * b + hh
                    r = kk % 2
                    for g in range(6):
                        n, p, f = RS.take()
                        for k in range(2):
                            pe = T(lambda e, k=k, g=g, p=p, r=r: e.matmul(
                                p[:, :], wh[:, r, k, 128 * g:128 * g + 128], hT[:, k, :], start=(k == 0),
                                stop=(k == 1)), hr, whm[kk], f)
                        if g < 4:
                            v = V(lambda e, g=g, p=p, r=r: e.tensor_tensor(qs[:, r, g, :], p[:, :], rot[:, 0, :],
                                                                           ALU.mult), pe, qk_free[r])
                        else:
                            v = V(lambda e, g=g, p=p: e.tensor_tensor(t1[:, g - 4, :], p[:, :], rot[:, g - 3, :],
                                                                      ALU.mult), pe)
                        RS.free[n] = v
                    whfree[r] = pe
                    if kk + 2 < 64:
                        load(kk + 2)
                    m_q[hh] = V(lambda e, r=r: e.tensor_tensor(ks[:, r, :], t1[:, 0, :], t1[:, 1, :], ALU.add))

                jobs = [(hh, i, g) for hh in range(8) for i in range(4) for g in range(4)]
                N = len(jobs)
                base = len(hist)
                hist.extend(dict() for _ in jobs)
                grp = {}

                def score(t):
                    hh, i, g = jobs[t]
                    if i == 0 and g == 0:
                        project(hh)
                    s, u = hist[base + t], base + t
                    r = u % 3
                    kr = (8 * b + hh) % 2
                    nk = 128 * (i + 1)
                    n, p, f = RS.take()
                    s["pe"] = T(lambda e: e.matmul(p[:, 0:nk], qs[:, kr, g, 128 * i:128 * i + 128], ks[:, kr, 0:nk],
                                                   start=True, stop=True), m_q[hh], f)
                    if i == 3 and g == 3:
                        qk_free[kr] = s["pe"]
                    s["v"] = RS.free[n] = V(lambda e: e.tensor_tensor_reduce(
                        fm[:, r, 0:nk], p[:, 0:nk], causal[:, 512 - nk:512], -S2, BIG, ALU.add, ALU.min,
                        bs[:, u % 4:u % 4 + 1]), s["pe"], past(u - 3, "exp"))
                    s["exp"] = A(lambda e: e.activation(ef[:, u % 4, 0:nk], fm[:, r, 0:nk], ACT.Exp,
                                                        bias=bs[:, u % 4:u % 4 + 1], scale=-1.0,
                                                        accum_out=zz[:, (u // 4) % 4, g:g + 1]),
                                 s["v"], past(u - 4, "tr"), z_free[(u // 4) % 4])

                def norm(t):
                    hh, i, g = jobs[t]
                    s, u = hist[base + t], base + t
                    zi = (u // 4) % 4
                    z_free[zi] = V(lambda e: e.reciprocal(zr[:, zi, g:g + 1], zz[:, zi, g:g + 1]), s["exp"])
                    s["p"] = V(lambda e: e.tensor_scalar(ef[:, u % 4, 0:128 * (i + 1)], ef[:, u % 4, 0:128 * (i + 1)],
                                                         zr[:, zi, g:g + 1], None, ALU.mult))

                def turn(t):
                    hh, i, g = jobs[t]
                    s, u = hist[base + t], base + t
                    nk = 128 * (i + 1)
                    n, p, f = RF.take()
                    for j in range(i + 1):
                        s["tr"] = T(lambda e: e.transpose(p[:, 128 * j:128 * j + 128],
                                                          ef[:, u % 4, 128 * j:128 * j + 128], ident[:]), s["p"], f)
                    s["ev"] = RF.free[n] = evac(A if u % 4 else V, tf[:, (u // 4) % 2, 0:i + 1, g, :],
                                                p[:, 0:nk].rearrange("p (j q) -> p j q", q=128), s["tr"],
                                                past(u - g - 5, "pv"))

                def apply(t):
                    hh, i, g = jobs[t]
                    s, u = hist[base + t], base + t
                    ro = (u // 4) % 2
                    n, p, f = RO.take()
                    for j in range(i + 1):
                        s["pv"] = T(lambda e: e.matmul(p[:, :], vt[:, j, 64 * hh:64 * hh + 64],
                                                       tf[:, ro, j, :, :].rearrange("p g q -> p (g q)"),
                                                       start=(j == 0), stop=(j == i)),
                                    [hist[u - d]["ev"] for d in range(4)], m_v, f)
                    pg = p[:, :].rearrange("p (k a q) -> p k a q", k=2, a=2)
                    v = V(lambda e: e.tensor_copy(oT[0:64, ro, :, :], pg[:, :, 0, :]), s["pv"], oT_free[ro])
                    a = V(lambda e: e.tensor_copy(oT[64:128, ro, :, :], pg[:, :, 1, :]))
                    s["oT"] = RO.free[n] = a

                def out_proj(t):
                    hh, i, g = jobs[t]
                    s, u = hist[base + t], base + t
                    ro = (u // 4) % 2
                    for k in range(2):
                        first = hh == 0 and k == 0 and i % 2 == 0
                        pe = T(lambda e, k=k, first=first: e.matmul(
                            Y[i], oT[:, ro, k, :], wo[:, 2 * hh + k, :],
                            start=first, stop=(hh == 7 and k == 1), skip_group_check=True), s["oT"], y_free)
                    oT_free[ro] = pe
                    return pe

                for t in range(N + 8):
                    if t < N:
                        score(t)
                    if 1 <= t < N + 1:
                        norm(t - 1)
                    if 3 <= t < N + 3:
                        turn(t - 3)
                    if 4 <= t < N + 4 and (t - 4) % 4 == 3:
                        apply(t - 4)
                    if 6 <= t < N + 6 and (t - 6) % 4 == 3:
                        pe = out_proj(t - 6)
                    if 8 <= t < 64 and t % 8 == 2:
                        next(behind, None)
                    if t == 64:
                        for _ in behind:
                            pass
                    if 70 <= t < 128 and t % 6 == 1:
                        next(ahead, None)
                for i in range(4):
                    v = V(lambda e: e.tensor_tensor(y2[:, b % 2, i, :], y2[:, b % 2, i, :], Y[i], ALU.add), pe)
                y_free = v
                for _ in ahead:
                    pass
                behind = after(b)
            for _ in behind:
                pass

        def phase_e(ctx, HT, RW):
            def sb(n, shape, dt=F32):
                return sbt(ctx, "e_" + n, shape, dt)

            wmod = sb("wmod", [128, 2, 768])
            w = SP.dma(wmod[:], D["wmod1b"], c_w)
            acc = sb("acc", [128, 32, 256])
            we = sb("we", [128, 3, 1536])
            sg = sb("sg", [128, 4, 512])
            hm = sb("hm", [128, 4, 2, 512])
            tmp = sb("tmp", [128, 256])
            wfree = [None] * 3
            wm = {}

            def load(ex):
                r = ex % 3
                wm[ex] = SP.dma(we[:, r, :], D["exp1"][ex], c_e[r], wfree[r])

            for ex in range(3):
                load(ex)
            V(lambda e: e.memset(acc[:], 0.0))
            RG = Ring([PS[:, i, :] for i in range(4)])
            RD = Ring([PS[:, 4 + i, :] for i in range(4)])
            jobs = [(ex, c) for ex in range(16) for c in range(8)]
            st = [dict() for _ in jobs]
            hist = []

            def up(t):
                ex, c = jobs[t]
                r, r4 = ex % 3, t % 4
                for m in range(2):
                    ps = []
                    for o in (0, 256):
                        n, p, f = RG.take()
                        for k in range(2):
                            c0 = 512 * k + o + 128 * m
                            pe = T(lambda e, k=k, c0=c0, p=p: e.matmul(
                                p[:, :], we[:, r, c0:c0 + 128], HT[:, k, 512 * c:512 * c + 512],
                                start=(k == 0), stop=(k == 1)), wm[ex], f)
                        ps.append((n, p, pe))
                    (n1, p1, e1), (n2, p2, e2) = ps
                    u = len(hist)
                    a = RG.free[n1] = A(lambda e, u=u, p1=p1: e.activation(sg[:, u % 4, :], p1[:, :], ACT.Silu), e1,
                                        hist[u - 4] if u >= 4 else None)
                    v = RG.free[n2] = V(lambda e, u=u, m=m, p2=p2: e.tensor_tensor(
                        hm[:, r4, m, :], sg[:, u % 4, :], p2[:, :], ALU.mult), a, e2,
                        st[t - 4]["pe"] if t >= 4 else None)
                    hist.append(v)
                st[t]["hm"] = v

            def down(t):
                ex, c = jobs[t]
                r, r4 = ex % 3, t % 4
                for i in range(4):
                    n, p, f = RD.take()
                    for k in range(2):
                        pe = T(lambda e, i=i, k=k, p=p: e.matmul(
                            p[:, 0:256], hm[:, r4, k, 128 * i:128 * i + 128],
                            we[:, r, 1024 + 256 * k:1280 + 256 * k], start=(k == 0), stop=(k == 1)), st[t]["hm"], f)
                    g = 4 * c + i
                    RD.free[n] = V(lambda e, p=p, g=g: e.scalar_tensor_tensor(
                        acc[:, g, :], p[:, 0:256], RW[:, g, ex:ex + 1], acc[:, g, :], ALU.mult, ALU.add), pe)
                st[t]["pe"] = pe
                if c == 7:
                    wfree[r] = pe
                    if ex + 3 < 16:
                        load(ex + 3)

            for t in range(len(jobs) + 1):
                if t < len(jobs):
                    up(t)
                if t:
                    down(t - 1)
            for b in range(8):
                mod_rows(1, b, wmod, w, RG)
                for i in range(4):
                    g = 4 * b + i
                    V(lambda e, g=g: e.tensor_tensor(tmp[:], acc[:, g, :], mb[:, 2, :], ALU.mult))
                    v = V(lambda e, g=g: e.tensor_tensor(X(g), X(g), tmp[:], ALU.add))
                SP.dma(xout[:, 4 * b:4 * b + 4, :], home["at"][:, 4 * b:4 * b + 4, :], c_o, v)

        with ExitStack() as ctx:
            phase_a(ctx)
        fence()
        Xs = sbt(top, "X", [128, 32, 256])
        m_x = SP.dma(Xs[:], xout, c_x)
        home.update(at=Xs, n=32, ready=lambda b: m_x)
        for phase in (phase_b, phase_c):
            with ExitStack() as ctx:
                phase(ctx)
            fence()
        with ExitStack() as keep:
            HT = sbt(keep, "HT", [128, 2, 4096])
            RW = sbt(keep, "RW", [128, 32, 16])
            with ExitStack() as ctx:
                phase_d(ctx, HT, RW)
            fence()
            with ExitStack() as ctx:
                phase_e(ctx, HT, RW)
            fence()


def layouts(I):
    d = {}

    def two(w):
        return np.ascontiguousarray(w.reshape(2, 128, -1).transpose(1, 0, 2))

    d["x"] = I["L0_attn_hidden_states"]
    d["c0"] = np.ascontiguousarray(I["L0_c"].T.reshape(2, 128, 8).transpose(1, 0, 2))
    d["c1"] = np.ascontiguousarray(I["L1_c"].T.reshape(2, 128, 8).transpose(1, 0, 2))
    for n in "01":
        d[f"wmod{n}a"], d[f"wmod{n}b"] = two(I[f"L{n}_wmod"][:, 0:768]), two(I[f"L{n}_wmod"][:, 768:1536])
    wqkv = I["L0_attn_w_qkv"]
    sw = np.arange(320) ^ 1
    d["wq0"] = two(np.concatenate([wqkv[:, 0:256], wqkv[:, sw[0:256]], wqkv[:, 256:384], wqkv[:, sw[256:320]]], 1))
    d["wg0"] = two(I["L0_attn_w_gate"])
    d["bg0"] = I["L0_attn_b_gate"].reshape(1, 96)
    d["wo0"] = two(I["L0_attn_w_out"])
    d["cw1"] = np.stack([I[f"L0_attn_{n}_cw1"].reshape(16, 8, 128).transpose(1, 0, 2) for n in "kv"], 1)
    d["kvpos"] = np.stack([I[f"L0_attn_{n}_pos"].transpose(2, 1, 0) for n in "kv"], 1)
    d["cb1"] = np.stack([I[f"L0_attn_{n}_cb1"] for n in "kv"], 1)
    d["cw2k"] = np.tile(I["L0_attn_k_cw2"], (1, 16))
    d["cb2k"] = np.tile(I["L0_attn_k_cb2"], 16).reshape(128, 1)
    d["cw2v"] = I["L0_attn_v_cw2"]
    d["cb2v"] = np.tile(I["L0_attn_v_cb2"][None], (128, 1))
    d["mck"] = np.tile(I["L0_attn_mem_ck"][:, 0, :].T, (16, 1))
    d["mcv"] = np.tile(I["L0_attn_mem_cv"].reshape(1, 8, 8), (128, 1, 1))
    d["tidx"] = I["L0_ffn_topk_idx"]
    d["tw"] = I["L0_ffn_topk_weight"]
    e = np.zeros((32, 128, 768), np.float32)
    g = I["L0_ffn_gate_weight"].transpose(0, 2, 1).reshape(32, 2, 128, 128)
    u = I["L0_ffn_up_weight"].transpose(0, 2, 1).reshape(32, 2, 128, 128)
    for kk in range(2):
        e[:, :, 256 * kk:256 * kk + 128] = g[:, kk]
        e[:, :, 256 * kk + 128:256 * kk + 256] = u[:, kk]
    e[:, :, 512:768] = I["L0_ffn_down_weight"].transpose(0, 2, 1)
    d["exp0"] = e
    d["wa1"] = two(I["L1_attn_c_attn_w"])
    ba = I["L1_attn_c_attn_b"]
    d["ba1"] = ba[0:512].reshape(4, 128).T
    d["bv1"] = ba[512:768].reshape(1, 256)
    d["wp1"] = two(I["L1_attn_c_proj_w"])
    d["bp1"] = I["L1_attn_c_proj_b"].reshape(1, 256)
    d["cg1"] = I["L1_attn_cam_gate"].reshape(128, 1)
    d["cw0"] = np.tile(I["L1_attn_cam_w0"].reshape(1, 1), (128, 1))
    d["cw1c"] = np.tile(I["L1_attn_cam_w1"].reshape(1, 1), (128, 1))
    d["lnw"] = np.tile(np.stack([I["L1_ffn_ln_w"], I["L1_ffn_ff_ln_w"]])[None], (128, 1, 1))
    wq = I["L1_ffn_wq"].reshape(256, 8, 4, 2, 32)
    wk = I["L1_ffn_wk"].reshape(256, 8, 2, 32)
    wh = np.zeros((256, 8, 6, 4, 32), np.float32)
    for s in range(2):
        wh[:, :, 0:4, s] = wq[:, :, :, s]
        wh[:, :, 0:4, 2 + s] = wq[:, :, :, 1 - s]
        for o in (0, 2):
            wh[:, :, 4, o + s] = wk[:, :, s]
            wh[:, :, 5, o + s] = wk[:, :, 1 - s]
    d["wh1"] = wh.reshape(2, 128, 8, 768).transpose(2, 1, 0, 3)
    d["wv1"] = two(I["L1_ffn_wv"])
    d["wo1"] = I["L1_ffn_wo"].reshape(16, 128, 256).transpose(1, 0, 2)
    d["wgr"] = two(I["L1_ffn_wg"])
    e = np.zeros((16, 128, 1536), np.float32)
    w1 = I["L1_ffn_w1"].reshape(16, 2, 128, 256)
    w3 = I["L1_ffn_w3"].reshape(16, 2, 128, 256)
    w2 = I["L1_ffn_w2"].reshape(16, 2, 128, 256)
    for kk in range(2):
        e[:, :, 512 * kk:512 * kk + 256] = w1[:, kk]
        e[:, :, 512 * kk + 256:512 * kk + 512] = w3[:, kk]
        e[:, :, 1024 + 256 * kk:1280 + 256 * kk] = w2[:, kk]
    d["exp1"] = e
    d.update(consts())
    return {k: np.ascontiguousarray(v) for k, v in d.items()}


def kernel(**inputs):
    import concourse.bacc as _bacc
    from concourse.bass_utils import run_bass_kernel_spmd as _run

    nc = _bacc.Bacc("TRN2", target_bir_lowering=False, num_devices=1)
    arrays, aps = {}, {}
    for name, a in layouts({k: np.asarray(v) for k, v in inputs.items()}).items():
        arrays["in_" + name] = a
        aps[name] = nc.dram_tensor("in_" + name, a.shape, mybir.dt.from_np(a.dtype), kind="ExternalInput").ap()
    aps["scr"] = nc.dram_tensor("scr", (3, 128, 3, 512), BF16, kind="Internal").ap()
    out = nc.dram_tensor("out_0", (8, 512, 256), F32, kind="ExternalOutput").ap()
    program(nc, aps, out)
    r = _run(nc, [arrays], core_ids=[0])
    return r.results[0]["out_0"]
```
